# Optimizing a Trainium2 kernel written in Bass

```python
import numpy as np
import jax
import jax.numpy as jnp

def _softmax(x, axis=-1):
    return jax.nn.softmax(x, axis=axis)

def _gelu(x):
    return jax.nn.gelu(x, approximate=True)

def _silu(x):
    return jax.nn.silu(x)

def _sigmoid(x):
    return jax.nn.sigmoid(x)

def _layernorm(x, axis=-1, eps=1e-05):
    m = jnp.mean(x, axis=axis, keepdims=True)
    v = jnp.var(x, axis=axis, keepdims=True)
    return (x - m) / jnp.sqrt(v + eps)

def _scatter_add(tgt, idx, src, axis=0):
    return tgt.at[idx].add(src)

def _segment_sum(src, seg, n):
    return jax.ops.segment_sum(src, seg, n)
kernel_name = 'mk_vit_tower_postln_d1_tok_img1024_r4_55f55a'

def setup_inputs(seed: int=0):
    np.random.seed(seed)
    _w = jnp.asarray

    def _rec_inputs():
        import jax
        import jax.numpy as jnp
        _rk = jax.random.key(seed)
        x = -0.00016672 + 0.999947 * jax.random.normal(jax.random.fold_in(_rk, 1), (64, 3, 96, 96), jnp.float32)
        return x
    x = _rec_inputs()

    def _L0_tok_setup():
        import jax, jax.numpy as jnp
        import numpy as np
        IMG = 96
        PATCH = 16
        C_IN = 3
        EMBED = 256
        NPH = IMG // PATCH
        NUM_PATCHES = NPH * NPH
        PATCH_DIM = PATCH * PATCH * C_IN
        key = jax.random.key(seed)
        k_x, k_w, k_b, k_cls, k_pos = jax.random.split(key, 5)
        x = jax.random.normal(k_x, (64, C_IN, IMG, IMG), dtype=jnp.float32)
        W = jax.random.normal(k_w, (EMBED, PATCH_DIM), dtype=jnp.float32) * (1.0 / np.sqrt(PATCH_DIM))
        b = jax.random.normal(k_b, (EMBED,), dtype=jnp.float32) * 0.01
        cls_token = jax.random.normal(k_cls, (1, 1, EMBED), dtype=jnp.float32) * 0.02
        pos_embed = jax.random.normal(k_pos, (1, NUM_PATCHES + 1, EMBED), dtype=jnp.float32) * 0.02
        return {'x': x, 'W': W, 'b': b, 'cls_token': cls_token, 'pos_embed': pos_embed}
    _L0_tok_all = _L0_tok_setup()
    _L0_tok_in = {k: v for k, v in _L0_tok_all.items() if k in ('W', 'b', 'cls_token', 'pos_embed')}
    del _L0_tok_all

    def _L0_attn_setup():
        import jax, jax.numpy as jnp
        import numpy as np
        DIM = 256
        HEADS = 8
        DIM_HEAD = 64
        DIM_INNER = HEADS * DIM_HEAD
        FRAC_GRAD = 0.5
        SCALE = DIM_HEAD ** (-0.5)

        def _forward(x, gamma, W_qkv, b_qkv, W_a, b_a, W_out, b_out):
            b, n, d = x.shape
            norm = jnp.clip(jnp.linalg.norm(x, axis=-1, keepdims=True), 1e-12)
            xn = x / norm * d ** 0.5 * gamma
            qkv = xn @ W_qkv + b_qkv
            qkv = qkv.reshape(b, n, 3, HEADS, DIM_HEAD)
            qkv = jnp.transpose(qkv, (2, 0, 3, 1, 4))
            q, k, v = (qkv[0], qkv[1], qkv[2])
            q = q * SCALE
            a = xn @ W_a + b_a
            a = a * FRAC_GRAD + jax.lax.stop_gradient(a) * (1.0 - FRAC_GRAD)
            a = a.reshape(b, n, HEADS, DIM_HEAD, 2)
            a = jnp.transpose(a, (0, 2, 1, 3, 4))
            re, im = (a[..., 0], a[..., 1])
            mag = jnp.sqrt(re * re + im * im)
            theta = jnp.arctan2(im, re)
            cum_log_r = jnp.cumsum(jax.nn.log_sigmoid(mag), axis=2)
            cum_theta = jnp.cumsum(theta, axis=2)
            a_cum_real = jnp.exp(cum_log_r) * jnp.cos(cum_theta)
            a_cum_real_inv = 1.0 / jnp.clip(a_cum_real, 1e-10)
            q = q * a_cum_real
            k = k * a_cum_real_inv
            sim = jnp.einsum('bhid,bhjd->bhij', q, k)
            causal_mask = jnp.triu(jnp.ones((n, n), dtype=bool), 1)
            attn = jnp.where(causal_mask, jnp.zeros((), sim.dtype), sim)
            out = jnp.einsum('bhij,bhjd->bhid', attn, v)
            out = jnp.transpose(out, (0, 2, 1, 3)).reshape(b, n, DIM_INNER)
            return out @ W_out + b_out
        key = jax.random.key(seed)
        ks = jax.random.split(key, 8)
        b, n = (1, 1024)
        x = jax.random.normal(ks[0], (b, n, DIM), dtype=jnp.float32)
        gamma = jnp.ones((DIM,), dtype=jnp.float32)
        W_qkv = jax.random.normal(ks[1], (DIM, DIM_INNER * 3), dtype=jnp.float32) * 0.02
        b_qkv = jnp.zeros((DIM_INNER * 3,), dtype=jnp.float32)
        W_a = jax.random.normal(ks[2], (DIM, DIM_INNER * 2), dtype=jnp.float32) * 0.02
        b_a = jnp.zeros((DIM_INNER * 2,), dtype=jnp.float32)
        W_out = jax.random.normal(ks[3], (DIM_INNER, DIM), dtype=jnp.float32) * 0.02
        b_out = jnp.zeros((DIM,), dtype=jnp.float32)
        return {'x': x, 'gamma': gamma, 'W_qkv': W_qkv, 'b_qkv': b_qkv, 'W_a': W_a, 'b_a': b_a, 'W_out': W_out, 'b_out': b_out}
    _L0_attn_all = _L0_attn_setup()
    _L0_attn_in = {k: v for k, v in _L0_attn_all.items() if k in ('gamma', 'W_qkv', 'b_qkv', 'W_a', 'b_a', 'W_out', 'b_out')}
    del _L0_attn_all

    def _L0_ffn_setup():
        import jax, jax.numpy as jnp
        import numpy as np
        T, Z, D_DIM = (8, 512, 256)
        N_EXP, P_SLOT, H = (64, 32, 256)
        LN_EPS = 1e-05
        key = jax.random.key(seed)
        k = jax.random.split(key, 5)
        s = 0.02
        return {'x': jax.random.normal(k[0], (T, Z, D_DIM), dtype=jnp.float32), 'phi_w': jax.random.normal(k[1], (N_EXP * P_SLOT, D_DIM), dtype=jnp.float32) * s, 'phi_b': jax.random.normal(k[2], (N_EXP * P_SLOT,), dtype=jnp.float32) * s, 'expert_w': jax.random.normal(k[3], (N_EXP, D_DIM, H), dtype=jnp.float32) * s, 'expert_b': jax.random.normal(k[4], (N_EXP, H), dtype=jnp.float32) * s}
    _L0_ffn_all = _L0_ffn_setup()
    _L0_ffn_in = {k: v for k, v in _L0_ffn_all.items() if k in ('phi_w', 'phi_b', 'expert_w', 'expert_b')}
    del _L0_ffn_all
    return {'x': x, 'L0_tok_W': _L0_tok_in['W'], 'L0_tok_b': _L0_tok_in['b'], 'L0_tok_cls_token': _L0_tok_in['cls_token'], 'L0_tok_pos_embed': _L0_tok_in['pos_embed'], 'L0_attn_gamma': _L0_attn_in['gamma'], 'L0_attn_W_qkv': _L0_attn_in['W_qkv'], 'L0_attn_b_qkv': _L0_attn_in['b_qkv'], 'L0_attn_W_a': _L0_attn_in['W_a'], 'L0_attn_b_a': _L0_attn_in['b_a'], 'L0_attn_W_out': _L0_attn_in['W_out'], 'L0_attn_b_out': _L0_attn_in['b_out'], 'L0_ffn_phi_w': _L0_ffn_in['phi_w'], 'L0_ffn_phi_b': _L0_ffn_in['phi_b'], 'L0_ffn_expert_w': _L0_ffn_in['expert_w'], 'L0_ffn_expert_b': _L0_ffn_in['expert_b']}

def reference(x, L0_tok_W, L0_tok_b, L0_tok_cls_token, L0_tok_pos_embed, L0_attn_gamma, L0_attn_W_qkv, L0_attn_b_qkv, L0_attn_W_a, L0_attn_b_a, L0_attn_W_out, L0_attn_b_out, L0_ffn_phi_w, L0_ffn_phi_b, L0_ffn_expert_w, L0_ffn_expert_b):
    import jax
    import jax.numpy as jnp

    def _L0_tok_ref(x, W, b, cls_token, pos_embed):
        import jax, jax.numpy as jnp
        import numpy as np
        IMG = 96
        PATCH = 16
        C_IN = 3
        EMBED = 256
        NPH = IMG // PATCH
        NUM_PATCHES = NPH * NPH
        PATCH_DIM = PATCH * PATCH * C_IN
        B, C, H, Wd = x.shape
        nph, npw = (H // PATCH, Wd // PATCH)
        patches = x.reshape(B, C, nph, PATCH, npw, PATCH)
        patches = patches.transpose(0, 2, 4, 1, 3, 5)
        patches = patches.reshape(B, nph * npw, C * PATCH * PATCH)
        proj = jnp.einsum('bnd,ed->bne', patches, W) + b
        cls = jnp.broadcast_to(cls_token, (B, 1, cls_token.shape[-1]))
        out = jnp.concatenate([cls, proj], axis=1) + pos_embed
        return out

    def _L0_attn_ref(x, gamma, W_qkv, b_qkv, W_a, b_a, W_out, b_out):
        import jax, jax.numpy as jnp
        import numpy as np
        DIM = 256
        HEADS = 8
        DIM_HEAD = 64
        DIM_INNER = HEADS * DIM_HEAD
        FRAC_GRAD = 0.5
        SCALE = DIM_HEAD ** (-0.5)

        def _forward(x, gamma, W_qkv, b_qkv, W_a, b_a, W_out, b_out):
            b, n, d = x.shape
            norm = jnp.clip(jnp.linalg.norm(x, axis=-1, keepdims=True), 1e-12)
            xn = x / norm * d ** 0.5 * gamma
            qkv = xn @ W_qkv + b_qkv
            qkv = qkv.reshape(b, n, 3, HEADS, DIM_HEAD)
            qkv = jnp.transpose(qkv, (2, 0, 3, 1, 4))
            q, k, v = (qkv[0], qkv[1], qkv[2])
            q = q * SCALE
            a = xn @ W_a + b_a
            a = a * FRAC_GRAD + jax.lax.stop_gradient(a) * (1.0 - FRAC_GRAD)
            a = a.reshape(b, n, HEADS, DIM_HEAD, 2)
            a = jnp.transpose(a, (0, 2, 1, 3, 4))
            re, im = (a[..., 0], a[..., 1])
            mag = jnp.sqrt(re * re + im * im)
            theta = jnp.arctan2(im, re)
            cum_log_r = jnp.cumsum(jax.nn.log_sigmoid(mag), axis=2)
            cum_theta = jnp.cumsum(theta, axis=2)
            a_cum_real = jnp.exp(cum_log_r) * jnp.cos(cum_theta)
            a_cum_real_inv = 1.0 / jnp.clip(a_cum_real, 1e-10)
            q = q * a_cum_real
            k = k * a_cum_real_inv
            sim = jnp.einsum('bhid,bhjd->bhij', q, k)
            causal_mask = jnp.triu(jnp.ones((n, n), dtype=bool), 1)
            attn = jnp.where(causal_mask, jnp.zeros((), sim.dtype), sim)
            out = jnp.einsum('bhij,bhjd->bhid', attn, v)
            out = jnp.transpose(out, (0, 2, 1, 3)).reshape(b, n, DIM_INNER)
            return out @ W_out + b_out
        return _forward(x, gamma, W_qkv, b_qkv, W_a, b_a, W_out, b_out)

    def _L0_ffn_ref(x, phi_w, phi_b, expert_w, expert_b):
        import jax, jax.numpy as jnp
        import numpy as np
        T, Z, D_DIM = (8, 512, 256)
        N_EXP, P_SLOT, H = (64, 32, 256)
        LN_EPS = 1e-05
        t, z, d = x.shape
        n = expert_w.shape[0]
        p = phi_w.shape[0] // n
        logits = (jnp.einsum('tzd,ed->tze', x, phi_w) + phi_b).reshape(t, z, n, p)
        D = jax.nn.softmax(logits, axis=3)
        C = jax.nn.softmax(logits, axis=2)
        X_tilde = jnp.einsum('tznp,tzd->npd', D, x)
        X_tilde = jnp.clip(X_tilde, -33000.0, 65000.0)
        mu = jnp.mean(X_tilde, axis=-1, keepdims=True)
        var = jnp.mean(jnp.square(X_tilde - mu), axis=-1, keepdims=True)
        X_tilde = (X_tilde - mu) * jax.lax.rsqrt(var + LN_EPS)
        X_tilde = jnp.tanh(X_tilde)
        Y_tilde = jnp.einsum('npd,ndH->npH', X_tilde, expert_w) + expert_b[:, None, :]
        Y = jnp.einsum('tznp,npH->tzH', C, Y_tilde)
        return Y
    h = _L0_tok_ref(x, L0_tok_W, L0_tok_b, L0_tok_cls_token, L0_tok_pos_embed)
    h = _layernorm(h + _L0_attn_ref(h, L0_attn_gamma, L0_attn_W_qkv, L0_attn_b_qkv, L0_attn_W_a, L0_attn_b_a, L0_attn_W_out, L0_attn_b_out), axis=-1)
    h = _layernorm(h + _L0_ffn_ref(h, L0_ffn_phi_w, L0_ffn_phi_b, L0_ffn_expert_w, L0_ffn_expert_b), axis=-1)
    return h

_drawn_inputs = setup_inputs


def setup_inputs(seed=0):
    import zlib

    import numpy as np

    out = dict(_drawn_inputs(seed))
    spreads = {'L0_attn_gamma': (1.0, 0.2),
     'L0_attn_b_qkv': (0.0, 0.1),
     'L0_attn_b_a': (0.0, 0.1),
     'L0_attn_b_out': (0.0, 0.547)}
    factors = {'L0_ffn_phi_b': 31.358}
    for name, (base, spread) in spreads.items():
        noise = np.random.default_rng([zlib.crc32(name.encode()), seed]).standard_normal(out[name].shape)
        drawn = base * np.exp(spread * noise) if base else spread * noise
        out[name] = jnp.asarray(drawn.astype(out[name].dtype))
    for name, factor in factors.items():
        out[name] = (out[name] * factor).astype(out[name].dtype)
    return out
```

```python
import concourse.bass as bass
from concourse import mybir
from contextlib import ExitStack
import math


def vit_tower_kernel(nc, x, tok_w, tok_b, cls_token, pos_embed, gamma, w_qkv, b_qkv, w_a, b_a,
                     w_out, b_out, phi_w, phi_b, expert_w, expert_b, out):
    f32, bf16 = mybir.dt.float32, mybir.dt.bfloat16
    ALU, ACT, AX = mybir.AluOpType, mybir.ActivationFunctionType, mybir.AxisListType
    ds = bass.ds

    NP = 128
    BANK = 512
    IMGS, CIN, IMG, _ = x.shape
    D = tok_w.shape[0]
    T = pos_embed.shape[1]
    PATCH = 16
    SIDE = IMG // PATCH
    KD = D // NP
    TOK = IMGS * T
    KC = CIN * PATCH * PATCH // NP
    XQ = 4
    XB = IMGS // XQ
    XP = XB * SIDE
    PH = SIDE // 2
    INNER = w_out.shape[0]
    NC = INNER // NP
    DH = 64
    GI = 3
    GT = GI * T
    NG = -(-IMGS // GI)
    NPT = 6
    PT = 408
    TP = PT * NPT
    assert TP >= NG * GT and NG % 2 == 0
    NS = phi_w.shape[0]
    NE = expert_w.shape[0]
    SL = NS // NE
    SC = NS // NP
    EC = NP // SL
    HS = NS // 2
    HE = NE // 2
    TT = -(-TOK // NP)
    LASTR = TOK - (TT - 1) * NP
    assert TT % 2 == 1 and TP >= TT * NP
    EPS = 1e-5
    TINY = 2.0 ** -64
    NORM_SHIFT = 20

    ctx = ExitStack()
    with ctx:
        def sem(name):
            return ctx.enter_context(nc.semaphore(name))

        WORDS = 53200
        arena = ctx.enter_context(nc.sbuf_tensor("arena", [NP, WORDS], f32))
        PS = ctx.enter_context(nc.psum_tensor("PS", [NP, 8, BANK], f32))

        class Region:
            def __init__(self, start, end):
                self.at, self.end = start, end

            def take(self, *shape):
                n = math.prod(shape)
                a = arena[:, self.at:self.at + n]
                self.at += n
                assert self.at <= self.end, (self.at, self.end)
                if len(shape) == 1:
                    return a
                names = [f"d{i}" for i in range(len(shape))]
                return a.rearrange(f"p ({' '.join(names)}) -> p {' '.join(names)}",
                                   **{names[i]: shape[i] for i in range(1, len(shape))})

        keep = Region(0, WORDS)
        ident = keep.take(NP)
        ones = keep.take(NP)
        mask = keep.take(GT)
        gam = keep.take(KD)
        neghalf = keep.take(1)
        bias3 = keep.take((NS + INNER) // 2).bitcast(bf16)
        ones3 = keep.take(NP // 2).bitcast(bf16)
        zeros3 = keep.take(NP // 2).bitcast(bf16)
        wc = [keep.take(KD, 5, NP) for _ in range(2)]
        bc = [keep.take(5) for _ in range(2)]
        xst = [keep.take(KD, GT) for _ in range(2)]
        kst = [keep.take(GT) for _ in range(2)]
        qst = [keep.take(GT) for _ in range(2)]
        vst = [keep.take(NP) for _ in range(2)]
        sraw = [keep.take(2, GT) for _ in range(2)]
        smk = [keep.take(2, GT) for _ in range(2)]
        stat = [keep.take(4) for _ in range(2)]
        bn6 = [keep.take(6) for _ in range(2)]
        scan1 = keep.take(2, IMGS)
        scan2 = keep.take(2, IMGS)
        h0T_at = keep.at
        h0T = keep.take(KD, TP)
        outT_at = keep.at
        outT = keep.take(NC, TP)
        xnT_at = keep.at
        xnT = keep.take(KD, TP)
        big_at = keep.at

        ra = Region(big_at, WORDS)
        xnat = [ra.take(CIN, PATCH, IMG) for _ in range(2)]
        patchT = [ra.take(KC, SIDE, XP) for _ in range(2)]
        tokW = ra.take(KD, KC * NP)
        tokWT = ra.take(KC, D)
        pos_nat = ra.take(D)
        posT = ra.take(KD, T)
        pos_add = ra.take(D)
        b3f = ra.take(NS + INNER)
        b3h = ra.take((NS + INNER) // 2).bitcast(bf16)
        xord = [Region(xnT_at, big_at).take(KC, SIDE, NP), Region(outT_at, xnT_at).take(KC, SIDE, NP)]
        rn = Region(outT_at, xnT_at)
        nsq = [rn.take(KD, PT) for _ in range(2)]
        nx = [rn.take(PT) for _ in range(2)]
        nl = [rn.take(PT) for _ in range(2)]
        nr = [rn.take(PT) for _ in range(2)]
        nt = [rn.take(PT) for _ in range(2)]
        rb = Region(big_at, WORDS)
        pha = rb.take(3, TP)
        cum = rb.take(2, TP)
        mag = rb.take(2, TP)
        inv = cum[:, 1]
        qT = [rb.take(TP) for _ in range(2)]
        kT = [rb.take(TP) for _ in range(2)]
        rc = Region(big_at, WORDS)
        phiT = rc.take(KD, NS)
        phi_nat = rc.take(SC, D)
        xs = phi_nat
        wo = rc.take(NC, D)
        bo = rc.take(D)
        h1 = rc.take(TT, D)
        h1T = rc.take(KD, TP)
        ost = [rc.take(NC, NP) for _ in range(2)]
        hst = [rc.take(KD, NP) for _ in range(2)]
        yst = [rc.take(D) for _ in range(2)]
        hn = [rc.take(D) for _ in range(2)]
        chunk_sel = rc.take(NP)
        smx = rc.take(NE)
        ssum = [rc.take(HE) for _ in range(2)]
        est = rc.take(SC, 5)
        ebn = rc.take(SC, 6)
        xtT = [rc.take(KD, NP) for _ in range(2)]
        rd = Region(xnT_at, big_at)
        dl = [rd.take(HS) for _ in range(2)]
        dn = [rd.take(HS) for _ in range(2)]
        yt = Region(xnT_at, big_at).take(SC, D)
        rf = Region(h0T_at, xnT_at)
        WEB = 5
        we = [rf.take(KD, EC, D) for _ in range(WEB)]
        eb = rf.take(SC, D)
        rg = Region(h0T_at, xnT_at)
        cl = [rg.take(NS) for _ in range(2)]
        cn = [rg.take(NS) for _ in range(2)]
        ct = [rg.take(SC, NP) for _ in range(2)]

        waited = sem("waited")
        d_tokw, d_pos, d_gam, d_b3 = sem("d_tokw"), sem("d_pos"), sem("d_gam"), sem("d_b3")
        d_x = [sem(f"d_x{i}") for i in range(2)]
        d_wc = [sem(f"d_wc{i}") for i in range(2)]
        d_wo, d_phi, d_eb = sem("d_wo"), sem("d_phi"), sem("d_eb")
        d_ost = [sem(f"d_ost{i}") for i in range(2)]
        d_hst = [sem(f"d_hst{i}") for i in range(2)]
        d_we = [sem(f"d_we{i}") for i in range(WEB)]
        d_st = [sem(f"d_st{i}") for i in range(2)]
        s_const, s_pool, s_act, s_setup, s_pad = sem("s_const"), sem("s_pool"), sem("s_act"), sem("s_setup"), sem("s_pad")
        wt_tr, wt_cp, pos_pre, pos_tr, pos_cp = sem("wt_tr"), sem("wt_cp"), sem("pos_pre"), sem("pos_tr"), sem("pos_cp")
        x_ord = [sem(f"x_ord_{name}") for name in ("act", "dve", "pool")]
        xt_tr, xt_act, xt_dve = sem("xt_tr"), sem("xt_act"), sem("xt_dve")
        pt_mm, h0_cp, h0_cls = sem("pt_mm"), sem("h0_cp"), sem("h0_cls")
        n_sq, n_mm, n_mx, n_ln, n_rs, n_nw, n_xn = (sem(s) for s in ("n_sq", "n_mm", "n_mx", "n_ln", "n_rs", "n_nw", "n_xn"))
        pj_mm, pj_cp = sem("pj_mm"), sem("pj_cp")
        c_chain, c_m2, c_ln, c_t, c_s, c_mx, c_inv, c_qk, c_nw = (
            sem(s) for s in ("c_chain", "c_m2", "c_ln", "c_t", "c_s", "c_mx", "c_inv", "c_qk", "c_nw"))
        sc_step = sem("sc_step")
        a_st, a_v, a_s, a_vcp, a_scp, a_mk, a_o, a_ocp = (
            sem(s) for s in ("a_st", "a_v", "a_s", "a_vcp", "a_scp", "a_mk", "a_o", "a_ocp"))
        ph_tr, ph_cp = sem("ph_tr"), sem("ph_cp")
        o_mm, o_y, o_bn, o_ve, o_rs, o_h, o_hc, o_tr, o_tc = (
            sem(s) for s in ("o_mm", "o_y", "o_bn", "o_ve", "o_rs", "o_h", "o_hc", "o_tr", "o_tc"))
        m_lg, m_max, m_sub, m_exp, m_sum, m_rc, m_dn, m_x, x_cp = (
            sem(s) for s in ("m_lg", "m_max", "m_sub", "m_exp", "m_sum", "m_rc", "m_dn", "m_x", "x_cp"))
        e_bn, e_ve, e_rs, e_nb, e_th, e_tr, e_tc, e_mm, e_cp = (
            sem(s) for s in ("e_bn", "e_ve", "e_rs", "e_nb", "e_th", "e_tr", "e_tc", "e_mm", "e_cp"))
        f_lg, f_max, f_sub, f_exp, f_sum, f_rc, f_cn, f_tr, f_tc, f_y, f_yb, f_bn, f_ve, f_rs, f_o = (
            sem(s) for s in ("f_lg", "f_max", "f_sub", "f_exp", "f_sum", "f_rc", "f_cn", "f_tr", "f_tc", "f_y", "f_yb",
                             "f_bn", "f_ve", "f_rs", "f_o"))
        CREDITS = [(xt_tr, 24), (xt_act, 2), (xt_dve, 2), (pt_mm, 8), (h0_cp, 4), (n_mm, 2), (n_mx, 2), (pj_cp, 4),
                   (a_v, 2), (a_s, 2), (a_vcp, 1), (a_scp, 1), (a_mk, 4), (a_o, 2), (a_ocp, 1),
                   (o_mm, 2), (o_y, 2), (o_hc, 2), (o_tr, 2), (o_tc, 2),
                   (m_lg, 2), (m_sub, 2), (m_dn, 2), (m_x, 2), (e_tc, 2), (e_mm, 2), (e_cp, 2),
                   (f_lg, 2), (f_sub, 1), (f_cn, 4), (f_tr, 8), (f_tc, 2), (f_y, 2), (f_yb, 2),
                   (d_st[0], 16), (d_st[1], 16)]

        def wait_apart(eng, semaphore, value):
            eng.wait_ge(semaphore, value)
            eng.sem_inc(waited, 1)

        def link(eng, ins, semaphore, value):
            ins.then_inc(semaphore, 1)
            eng.wait_ge(semaphore, value)

        def staggered(eng, n, front, back):
            front(0, 0, 0)
            with eng.Fori(0, (n - 1) // 2) as i:
                front(2 * i + 1, 1, i)
                back(2 * i, 0, i)
                front(2 * i + 2, 0, i + 1)
                back(2 * i + 1, 1, i)
            if n % 2 == 0:
                front(n - 1, 1, n // 2 - 1)
                back(n - 2, 0, n // 2 - 1)
            back(n - 1, (n - 1) % 2, (n - 1) // 2)

        def tiles(eng, n, body):
            with eng.Fori(0, n // 2) as i:
                body(2 * i, 0, i)
                body(2 * i + 1, 1, i)
            if n % 2:
                body(n - 1, 0, n // 2)

        def by_token(a):
            return a[:, :, 0:TOK].rearrange("p r (b t) -> p r t b", t=T)

        def patch_order(eng, copy, q, par, d, who):
            eng.wait_ge(d_x[par], 16 * CIN * (d + 1))
            wait_apart(eng, xt_tr, q * (2 * KC) + 12)
            for kc in (2 * who, 2 * who + 1):
                src = xnat[par][0:XP, kc // 2, 8 * (kc % 2):8 * (kc % 2) + 8].rearrange("p i (w j) -> p w i j", j=PATCH)
                copy(xord[par][0:XP, kc].rearrange("p w (i j) -> p w i j", j=PATCH), src).then_inc(x_ord[who], 1)

        block = ctx.enter_context(nc.Block())

        @block.sync
        def _(sp):
            sp.dma_start(tokW, tok_w.rearrange("(e p) k -> p e k", p=NP)).then_inc(d_tokw, 16)
            sp.dma_start(pos_nat[0:T], pos_embed[0]).then_inc(d_pos, 16)
            sp.dma_start(pos_add[0:1], cls_token[0]).then_inc(d_pos, 16)
            sp.dma_start(pos_add[1:T], tok_b.rearrange("(a e) -> a e", a=1).to_broadcast([T - 1, D])).then_inc(d_pos, 16)
            xv = x.rearrange("b c (ph i) w -> b ph c (i w)", ph=SIDE)

            def load_x(q, par, d=None):
                for c in range(CIN):
                    sp.dma_start(xnat[par][0:XP, c].rearrange("p i w -> p (i w)"),
                                 xv[q * XB:(q + 1) * XB, :, c, :]).then_inc(d_x[par], 16)

            load_x(0, 0)
            load_x(1, 1)
            sp.dma_start(gam, gamma.rearrange("(k p) -> p k", p=NP), allow_slow_non_contiguous=True).then_inc(d_gam, 16)
            sp.wait_ge(s_const, 1)
            for r in range(3):
                sp.dma_start(b3f[32 * r:32 * r + 1, 0:NS], phi_b.rearrange("(a n) -> a n", a=1)).then_inc(d_b3, 16)
                sp.dma_start(b3f[32 * r:32 * r + 1, NS:NS + INNER],
                             b_qkv[2 * INNER:3 * INNER].rearrange("(a n) -> a n", a=1)).then_inc(d_b3, 16)

            def load_wc(c):
                par = c % 2
                for k in range(KD):
                    sp.dma_start(wc[par][:, k, 0:3, :],
                                 w_qkv[k * NP:(k + 1) * NP, :].rearrange("p (s n) -> p s n", s=3)[:, :, c * NP:(c + 1) * NP]
                                 ).then_inc(d_wc[par], 16)
                sp.dma_start(wc[par][:, :, 3:5, :].rearrange("p k s n -> p k (s n)"),
                             w_a.rearrange("(k p) n -> p k n", p=NP)[:, :, c * 2 * NP:(c + 1) * 2 * NP]
                             ).then_inc(d_wc[par], 16)
                sp.dma_start(bc[par][:, 0:3], b_qkv.rearrange("(s c p) -> c p s", s=3, p=NP)[c], allow_slow_non_contiguous=True).then_inc(d_wc[par], 16)
                sp.dma_start(bc[par][:, 3:5], b_a.rearrange("(c p two) -> c p two", two=2, p=NP)[c], allow_slow_non_contiguous=True).then_inc(d_wc[par], 16)

            load_wc(0)
            load_wc(1)
            for q in range(2, XQ):
                for done in x_ord:
                    sp.wait_ge(done, 2 * (q - 1))
                load_x(q, q % 2)
            for c in range(2, NC):
                sp.wait_ge(a_v, 2 + NG * (c - 1))
                sp.wait_ge(pj_cp, 4 + 4 * NPT * (c - 1))
                load_wc(c)
            sp.wait_ge(c_qk, 2 * NC)
            sp.dma_start(phi_nat, phi_w.rearrange("(c p) d -> p c d", p=NP)).then_inc(d_phi, 16)
            sp.dma_start(wo, w_out.rearrange("(c p) d -> p c d", p=NP)).then_inc(d_wo, 16)
            sp.dma_start(bo, b_out.rearrange("(a n) -> a n", a=1).to_broadcast([NP, D])).then_inc(d_wo, 16)

            sp.wait_ge(a_ocp, 1 + NC * NG)

            def copy_out(t, par, d=None):
                sp.wait_ge(o_mm, t + 1)
                sp.dma_start(ost[par], outT[:, :, ds(t * NP, NP)]).then_inc(d_ost[par], 16)
                sp.wait_ge(o_mm, t + 1)
                sp.dma_start(hst[par], h0T[:, :, ds(t * NP, NP)]).then_inc(d_ost[par], 16)

            tiles(sp, TT, copy_out)

            sp.wait_ge(o_mm, 2 + TT)
            sp.wait_ge(s_pad, 1)

            def load_we(c):
                for k in range(KD):
                    sp.dma_start(we[c % WEB][:, k],
                                 expert_w[c * EC:(c + 1) * EC, k * NP:(k + 1) * NP, :].rearrange("e p h -> p e h")
                                 ).then_inc(d_we[c % WEB], 16)

            sp.wait_ge(d_ost[0], 32 * (TT // 2 + 1))
            sp.wait_ge(d_ost[1], 32 * (TT // 2))
            for c in range(WEB):
                load_we(c)
            sp.dma_start(eb[0:EC], expert_b.rearrange("(c e) d -> e c d", e=EC)).then_inc(d_eb, 16)
            for half in range(2):
                base = half * TT
                sp.wait_ge(m_lg, 2 + base)

                def copy_h1(t, par, d=None):
                    if half == 0:
                        wait_apart(sp, o_tc, t + 3)
                    sp.wait_ge(m_lg, t + base + 1)
                    sp.dma_start(hst[par], h1T[:, :, ds(t * NP, NP)]).then_inc(d_hst[par], 16)

                tiles(sp, TT, copy_h1)
            for c in range(WEB, SC):
                sp.wait_ge(e_mm, 2 + c - WEB + 1)
                load_we(c)
            sp.wait_ge(m_lg, 2 + 2 * TT)

            def copy_f(t, par, d=None):
                sp.wait_ge(f_lg, t + 1)
                sp.dma_start(hst[par], h1T[:, :, ds(t * NP, NP)]).then_inc(d_hst[par], 16)

            def store(t, par, rows=NP):
                sp.wait_ge(f_o, t + 1)
                sp.dma_start(out[ds(t * NP, rows), :], hn[par][0:rows]).then_inc(d_st[par], 16)

            copy_f(0, 0)
            copy_f(1, 1)
            with sp.Fori(0, TT // 2 - 1) as i:
                copy_f(2 * i + 2, 0)
                store(2 * i, 0)
                copy_f(2 * i + 3, 1)
                store(2 * i + 1, 1)
            copy_f(TT - 1, 0)
            store(TT - 3, 0)
            store(TT - 2, 1)
            store(TT - 1, 0, LASTR)
            sp.wait_ge(d_st[0], 16 + 16 * (TT // 2 + 1))
            sp.wait_ge(d_st[1], 16 + 16 * (TT // 2))

        @block.gpsimd
        def _(pool):
            g = nc.gpsimd
            for semaphore, n in CREDITS:
                pool.sem_inc(semaphore, n)
            g.memset(b3f, 0.0).then_inc(s_const, 1)
            g.memset(ident, 0.0).then_inc(s_pool, 1)
            g.memset(mask, float(DH) ** -0.5).then_inc(s_pool, 1)
            pool.wait_ge(s_pool, 2)
            g.affine_select(out=ident, in_=ident, compare_op=ALU.not_equal, fill=1.0, base=0,
                            pattern=[[-1, NP]], channel_multiplier=1).then_inc(s_const, 1)
            g.memset(bias3, 0.0).then_inc(s_const, 1)
            g.memset(ones3, 1.0).then_inc(s_const, 1)
            g.memset(zeros3, 0.0).then_inc(s_const, 1)
            g.memset(ones, 1.0).then_inc(s_const, 1)
            g.memset(neghalf, -0.5).then_inc(s_const, 1)
            for k in range(KD):
                g.memset(h0T[:, k, TOK:TP], 0.0).then_inc(s_const, 1)
            g.affine_select(out=mask, in_=mask, compare_op=ALU.is_ge, fill=0.0, base=0,
                            pattern=[[1, GT]], channel_multiplier=-1).then_inc(s_pool, 1)
            pool.wait_ge(s_pool, 3)
            m3 = mask.rearrange("p (b t) -> p b t", t=T)
            g.affine_select(out=m3, in_=m3, compare_op=ALU.is_ge, fill=0.0, base=0,
                            pattern=[[-T, GI], [0, T]], channel_multiplier=1).then_inc(s_pool, 1)
            pool.wait_ge(s_pool, 4)

            tiles(pool, XQ, lambda q, par, d: patch_order(pool, g.tensor_copy, q, par, d, 2))

            pool.wait_ge(n_xn, KD * NPT)
            for c in range(NC):
                pool.wait_ge(c_qk, 2 * (c + 1))
                base = c * NG

                def stage(gi, par, d=None):
                    n = gi + base
                    pool.wait_ge(a_v, n + 1)
                    g.tensor_copy(xst[par], xnT[:, :, ds(gi * GT, GT)]).then_inc(a_st, 1)
                    pool.wait_ge(a_s, n + 1)
                    g.tensor_copy(kst[par], kT[c % 2][:, ds(gi * GT, GT)]).then_inc(a_st, 1)
                    g.tensor_copy(qst[par], qT[c % 2][:, ds(gi * GT, GT)]).then_inc(a_st, 1)

                def apply_mask(gi, par, d=None):
                    n = gi + base
                    pool.wait_ge(a_scp, n + 2)
                    pool.wait_ge(a_o, n + 1)
                    for h in range(2):
                        g.tensor_tensor(smk[par][0:GT, h], sraw[par][0:GT, h], mask[0:GT], ALU.mult).then_inc(a_mk, 1)

                staggered(pool, NG, stage, apply_mask)

            pool.wait_ge(a_ocp, 1 + NC * NG)
            g.memset(h1[LASTR:NP, TT - 1], 0.0).then_inc(s_pool, 1)
            pool.wait_ge(s_pool, 5)
            g.memset(h1T[:, :, TOK:TP], 0.0).then_inc(s_pool, 1)
            g.memset(chunk_sel, 1.0).then_inc(s_pool, 1)
            pool.wait_ge(s_pool, 7)
            sel3 = chunk_sel.rearrange("p (e s) -> p e s", s=SL)
            g.affine_select(out=sel3, in_=sel3, compare_op=ALU.is_equal, fill=0.0, base=0,
                            pattern=[[-1, EC], [0, SL]], channel_multiplier=1).then_inc(s_pool, 1)
            pool.wait_ge(s_pool, 8)
            pool.sem_inc(s_pad, 1)

            def out_rstd(t, par, d=None):
                pool.wait_ge(o_ve, t + 1)
                g.tensor_tensor(stat[par][:, 3:4], stat[par][:, 2:3], neghalf, ALU.pow).then_inc(o_rs, 1)

            tiles(pool, TT, out_rstd)

            for half in range(2):
                base = half * TT
                pool.wait_ge(m_x, 2 + base)

                def normalise(t, par, d=None):
                    n = t + base
                    pool.wait_ge(m_rc, n + 1)
                    pool.wait_ge(m_x, n + 1)
                    g.tensor_tensor(dn[par].rearrange("p (n s) -> p n s", s=SL),
                                    dl[par].rearrange("p (n s) -> p n s", s=SL),
                                    ssum[par].unsqueeze(2).to_broadcast([NP, HE, SL]),
                                    ALU.mult).then_inc(m_dn, 1)

                tiles(pool, TT, normalise)

            pool.wait_ge(e_ve, 1)
            g.tensor_tensor(est[:, :, 3], est[:, :, 2], neghalf.to_broadcast([NP, SC]), ALU.pow).then_inc(e_rs, 1)

            pool.wait_ge(e_mm, 2 + SC)

            def combine_norm(t, par, d=None):
                pool.wait_ge(f_rc, t + 1)
                pool.wait_ge(f_tr, 4 * t + 4)
                for h in range(2):
                    part = slice(h * HS, (h + 1) * HS)
                    g.tensor_tensor(cn[par][:, part].rearrange("p (n s) -> p n s", s=SL),
                                    cl[par][:, part].rearrange("p (n s) -> p n s", s=SL),
                                    ssum[par].unsqueeze(1).to_broadcast([NP, HE, SL]),
                                    ALU.mult).then_inc(f_cn, 1)

            def combine_rstd(t, par, d=None):
                pool.wait_ge(f_ve, t + 1)
                g.tensor_tensor(stat[par][:, 3:4], stat[par][:, 2:3], neghalf, ALU.pow).then_inc(f_rs, 1)

            combine_norm(0, 0)
            with pool.Fori(0, TT // 2) as i:
                combine_rstd(2 * i, 0)
                combine_norm(2 * i + 1, 1)
                combine_rstd(2 * i + 1, 1)
                combine_norm(2 * i + 2, 0)
            combine_rstd(TT - 1, 0)

        @block.scalar
        def _(act):
            a = nc.scalar
            for j in range(3):
                act.wait_ge(wt_tr, j + 1)
                a.activation(tokWT[:, 2 * j:2 * j + 2, :].rearrange("p k e -> p (k e)"), PS[:, j, :], ACT.Copy
                             ).then_inc(wt_cp, 1)

            def patch_copies(q, par, d=None):
                act.wait_ge(pt_mm, 4 * q + 4)
                for u in range(0, 2 * KC, 2):
                    act.wait_ge(xt_tr, q * (2 * KC) + u + 25)
                    a.activation(patchT[par][:, u // 2, 0:PH, :].rearrange("p w r -> p (w r)"),
                                 PS[:, u % 4, 0:PH * XP], ACT.Copy).then_inc(xt_act, 1)

            def copy_act(dst, src):
                return a.activation(dst, src, ACT.Copy)

            staggered(act, XQ, lambda q, par, d: patch_order(act, copy_act, q, par, d, 0), patch_copies)

            act.wait_ge(h0_cp, 4 + 4 * XQ)
            act.wait_ge(h0_cls, 1)
            act.wait_ge(s_const, 9)

            def norm_square(n, par, d=None):
                act.wait_ge(n_mm, n + 1)
                a.activation(nsq[par], h0T[:, :, ds(n * PT, PT)], ACT.Square).then_inc(n_sq, 1)

            def norm_rsqrt(n, par, d=None):
                act.wait_ge(n_mx, n + 3)
                a.activation(nl[par], nx[par], ACT.Ln, scale=2.0 ** NORM_SHIFT).then_inc(n_ln, 1)
                act.wait_ge(n_ln, n + 1)
                a.activation(nr[par], nl[par], ACT.Exp, scale=-0.5, bias=0.5 * NORM_SHIFT * math.log(2.0)
                             ).then_inc(n_rs, 1)

            staggered(act, NPT, norm_square, norm_rsqrt)

            def project_copies(c):
                par = c % 2
                act.wait_ge(d_wc[par], 80 * (c // 2 + 1))
                if c == 0:
                    act.wait_ge(n_xn, KD * NPT)
                else:
                    act.wait_ge(c_mx, c)
                    act.wait_ge(c_qk, 2 * c)
                if c >= 2:
                    act.wait_ge(a_o, 2 + NG * (c - 1))
                with act.Fori(0, NPT) as n:
                    cols = ds(n * PT, PT)
                    u0 = (n + c * NPT) * 4
                    for part in range(2):
                        act.wait_ge(pj_mm, u0 + part + 1)
                        a.activation(pha[:, part, cols], PS[:, part, 0:PT], ACT.Identity, bias=bc[par][:, 3 + part:4 + part]
                                     ).then_inc(s_act, 1)
                        a.activation(mag[:, part, cols], PS[:, part, 0:PT], ACT.Square, bias=bc[par][:, 3 + part:4 + part]
                                     ).then_inc(pj_cp, 1)
                    act.wait_ge(pj_mm, u0 + 3)
                    a.activation(qT[par][:, cols], PS[:, 2, 0:PT], ACT.Identity, bias=bc[par][:, 0:1]).then_inc(pj_cp, 1)
                    act.wait_ge(pj_mm, u0 + 4)
                    a.activation(kT[par][:, cols], PS[:, 3, 0:PT], ACT.Identity, bias=bc[par][:, 1:2]).then_inc(pj_cp, 1)

            def phasor_scale(c):
                s0 = 2 * NPT * (c + 1) + 4 * c
                act.wait_ge(c_m2, c + 1)
                a.activation(mag[:, 0], mag[:, 0], ACT.Ln).then_inc(s_act, 1)
                act.wait_ge(s_act, s0 + 1)
                a.activation(mag[:, 1], mag[:, 0], ACT.Exp, scale=0.5).then_inc(s_act, 1)
                act.wait_ge(s_act, s0 + 2)
                a.activation(mag[:, 1], mag[:, 1], ACT.Exp, scale=-1.0).then_inc(s_act, 1)
                act.wait_ge(s_act, s0 + 3)
                a.activation(mag[:, 1], mag[:, 1], ACT.Ln, bias=1.0).then_inc(c_ln, 1)
                act.wait_ge(c_t, c + 1)
                a.activation(mag[:, 0], mag[:, 0], ACT.Exp, scale=-1.0).then_inc(c_s, 1)

            def inverse(c):
                s0 = 2 * NPT * (c + 1) + 4 * c
                act.wait_ge(c_mx, c + 1)
                a.activation(mag[:, 1], mag[:, 0], ACT.Ln).then_inc(s_act, 1)
                act.wait_ge(s_act, s0 + 4)
                a.activation(mag[:, 1], mag[:, 1], ACT.Exp, scale=-1.0).then_inc(c_inv, 1)

            def attend_copies(c):
                base = c * NG

                def front(gi, par, d=None):
                    n = gi + base
                    act.wait_ge(a_v, n + 3)
                    act.wait_ge(a_o, n + 1)
                    a.activation(vst[par][0:GT], PS[0:GT, 4, 0:NP], ACT.Copy).then_inc(a_vcp, 1)
                    act.wait_ge(a_s, n + 3)
                    act.wait_ge(a_mk, 2 * n + 2)
                    a.activation(sraw[par][0:GT], PS[0:GT, 5:7, 0:GT], ACT.Copy).then_inc(a_scp, 1)

                def back(gi, par, d=None):
                    n = gi + base
                    act.wait_ge(a_o, n + 3)
                    a.activation(outT[:, c, ds(gi * GT, GT)], PS[:, 7, 0:GT], ACT.Copy).then_inc(a_ocp, 1)

                staggered(act, NG, front, back)

            for c in range(NC):
                project_copies(c)
                phasor_scale(c)
                if c:
                    attend_copies(c - 1)
                inverse(c)
            attend_copies(NC - 1)

            for j in range(2 * KD * 2):
                act.wait_ge(ph_tr, j + 1)
                k, s = j // 4, j % 4
                a.activation(phiT[:, k, s * BANK:(s + 1) * BANK], PS[:, s, :], ACT.Copy).then_inc(ph_cp, 1)

            def keep_h1(t, par, rows=NP):
                act.wait_ge(o_h, t + 1)
                a.activation(h1[0:rows, ds(t, 1), :], hn[par][0:rows].unsqueeze(1), ACT.Copy).then_inc(o_hc, 1)
                act.wait_ge(o_tr, t + 3)
                a.activation(h1T[:, :, ds(t * NP, rows)],
                             PS[:, 6 + par, 0:D].rearrange("p (k n) -> p k n", k=KD)[:, :, 0:rows], ACT.Copy
                             ).then_inc(o_tc, 1)

            act.wait_ge(s_pad, 1)
            with act.Fori(0, TT // 2) as i:
                keep_h1(2 * i, 0)
                keep_h1(2 * i + 1, 1)
            keep_h1(TT - 1, 0, LASTR)

            for half in range(2):
                def dispatch_exp(t, par, d=None):
                    act.wait_ge(m_sub, t + half * TT + 3)
                    a.activation(dl[par], dl[par], ACT.Exp).then_inc(m_exp, 1)

                tiles(act, TT, dispatch_exp)

            act.wait_ge(e_nb, 1)
            for j in range(SC):
                a.activation(xs[:, j], xs[:, j], ACT.Tanh, bias=est[:, j, 4:5], scale=est[:, j, 3:4]).then_inc(e_th, 1)
            for j in range(SC):
                act.wait_ge(e_tr, j + 1)
                act.wait_ge(e_mm, j + 1)
                a.activation(xtT[j % 2], PS[:, j % 2, 0:D].rearrange("p (k n) -> p k n", k=KD), ACT.Copy).then_inc(e_tc, 1)

            def combine_exp(t, par, d=None):
                act.wait_ge(f_sub, t + 2)
                a.activation(cl[par], cl[par], ACT.Exp).then_inc(f_exp, 1)

            def combine_copies(t, par, d=None):
                act.wait_ge(f_y, t + 1)
                for b in range(4):
                    act.wait_ge(f_tr, 4 * t + b + 9)
                    a.activation(ct[par][:, 4 * b:4 * b + 4, :],
                                 PS[:, 4 + b % 2, :].rearrange("p (j n) -> p j n", n=NP), ACT.Copy).then_inc(f_tc, 1)

            act.wait_ge(e_mm, 2 + SC)
            combine_exp(0, 0)
            with act.Fori(0, TT // 2) as i:
                combine_copies(2 * i, 0)
                combine_exp(2 * i + 1, 1)
                combine_copies(2 * i + 1, 1)
                combine_exp(2 * i + 2, 0)
            combine_copies(TT - 1, 0)

        @block.vector
        def _(dve):
            v = nc.vector
            dve.wait_ge(d_pos, 48)
            v.tensor_tensor(pos_nat[0:T], pos_nat[0:T], pos_add[0:T], ALU.add).then_inc(pos_pre, 1)
            dve.wait_ge(d_gam, 16)
            link(dve, v.tensor_scalar(gam, gam, math.sqrt(D), None, ALU.mult), s_setup, 1)
            dve.wait_ge(pos_tr, 1)
            v.tensor_copy(posT.rearrange("p k t -> p (k t)"), PS[:, 3, 0:KD * T]).then_inc(pos_cp, 1)
            dve.wait_ge(pos_cp, 1)

            def patch_copies(q, par, d=None):
                dve.wait_ge(pt_mm, 4 * q + 4)
                for u in range(1, 2 * KC, 2):
                    dve.wait_ge(xt_tr, q * (2 * KC) + u + 25)
                    v.tensor_copy(patchT[par][:, u // 2, PH:SIDE, :].rearrange("p w r -> p (w r)"),
                                  PS[:, u % 4, 0:PH * XP]).then_inc(xt_dve, 1)
                for j in range(4):
                    e, half = j // 2, j % 2
                    dve.wait_ge(pt_mm, 8 + 4 * q + j + 1)
                    src = PS[:, 4 + j, 0:PH * XP].rearrange("p (w b s) -> p s b w", w=PH, b=XB)
                    dst = h0T[:, e, ds(q * (XB * T), XB * T)].rearrange("p (b t) -> p b t", t=T)[:, :, 1:T] \
                        .rearrange("p b (s w) -> p s b w", s=SIDE)
                    add = posT[:, e, 1:T].rearrange("p (s w) -> p s w", s=SIDE)
                    for s in range(SIDE):
                        ins = v.tensor_tensor(dst[:, s, :, half * PH:(half + 1) * PH], src[:, s],
                                              add[:, s, half * PH:(half + 1) * PH].unsqueeze(1).to_broadcast([NP, XB, PH]),
                                              ALU.add)
                    ins.then_inc(h0_cp, 1)

            staggered(dve, XQ, lambda q, par, d: patch_order(dve, v.tensor_copy, q, par, d, 1), patch_copies)
            v.tensor_copy(h0T[:, :, 0:TOK].rearrange("p k (b t) -> p k b t", t=T)[:, :, :, 0],
                          posT[:, :, 0:1].to_broadcast([NP, KD, IMGS])).then_inc(h0_cls, 1)

            nb = NS + INNER
            dve.wait_ge(d_b3, 96)
            dve.wait_ge(s_const, 9)
            for r in range(3):
                row = slice(32 * r, 32 * r + 1)
                link(dve, v.tensor_copy(b3h[0:65, 0:nb], b3f[0:65]), s_setup, 2 + 3 * r)
                link(dve, v.tensor_copy(bias3[row, 0:nb], b3h[row, 0:nb]), s_setup, 3 + 3 * r)
                link(dve, v.tensor_tensor(b3f[0:65], b3f[0:65], b3h[0:65, 0:nb], ALU.subtract), s_setup, 4 + 3 * r)

            dve.wait_ge(h0_cls, 1)

            def norm_max(n, par, d=None):
                dve.wait_ge(n_mm, n + 3)
                v.tensor_scalar(nx[par], PS[:, par, 0:PT], 1e-24, None, ALU.max).then_inc(n_mx, 1)

            def norm_apply(n, par, d=None):
                dve.wait_ge(n_rs, n + 1)
                link(dve, v.tensor_tensor(nt[par], nr[par], nr[par], ALU.mult), n_nw, 3 * n + 1)
                link(dve, v.scalar_tensor_tensor(nt[par], nt[par], -0.5, nx[par], ALU.mult, ALU.mult), n_nw, 3 * n + 2)
                link(dve, v.scalar_tensor_tensor(nr[par], nt[par], 1.5, nr[par], ALU.add, ALU.mult), n_nw, 3 * n + 3)
                for k in range(KD):
                    v.scalar_tensor_tensor(xnT[:, k, ds(n * PT, PT)], h0T[:, k, ds(n * PT, PT)], gam[:, k:k + 1],
                                           nr[par], ALU.mult, ALU.mult).then_inc(n_xn, 1)

            staggered(dve, NPT, norm_max, norm_apply)

            dve.wait_ge(n_xn, KD * NPT)
            v.memset(cum[:, :, TOK:TP], 0.0).then_inc(s_setup, 1)
            dve.wait_ge(s_setup, 11)
            pt_, ct_ = by_token(pha), by_token(cum)
            CH = 7

            for c in range(NC):
                par = c % 2
                l0 = CH * c
                dve.wait_ge(pj_cp, 4 + 4 * NPT * (c + 1))
                link(dve, v.tensor_tensor(mag[:, 0], mag[:, 0], mag[:, 1], ALU.add), c_chain, l0 + 1)
                link(dve, v.tensor_scalar(mag[:, 1], mag[:, 0], TINY, math.sqrt(TINY), ALU.is_lt, ALU.mult), c_chain, l0 + 2)
                link(dve, v.tensor_tensor(pha[:, 0], pha[:, 0], mag[:, 1], ALU.add), c_chain, l0 + 3)
                v.tensor_scalar(mag[:, 0], mag[:, 0], TINY, None, ALU.max).then_inc(c_m2, 1)
                dve.wait_ge(c_ln, c + 1)
                v.scalar_tensor_tensor(mag[:, 0], mag[:, 0], 0.5, mag[:, 1], ALU.mult, ALU.add).then_inc(c_t, 1)
                dve.wait_ge(c_s, c + 1)
                link(dve, v.scalar_tensor_tensor(pha[:, 2], pha[:, 1], -1.0, mag[:, 0], ALU.mult, ALU.mult), c_chain, l0 + 4)
                v.tensor_tensor(pha[:, 0], pha[:, 0], mag[:, 0], ALU.mult).then_inc(c_chain, 1)
                v.tensor_tensor(pha[:, 1], pha[:, 1], mag[:, 0], ALU.mult).then_inc(c_chain, 1)
                dve.wait_ge(c_chain, l0 + 6)

                s0 = c * (1 + 3 * (T - 1))
                link(dve, v.tensor_copy(ct_[:, :, 0, :], pt_[:, 0:2, 0, :]), sc_step, s0 + 1)
                UN = 4
                with dve.Fori(0, (T - 1) // UN) as i:
                    for u in range(UN):
                        t = i * UN + (u + 1)
                        before = ct_[:, :, ds(i * UN + u, 1), :]
                        n = s0 + 1 + 3 * (i * UN + u)
                        v.tensor_tensor(scan1.unsqueeze(2), before,
                                        pt_[:, 0:1, ds(t, 1), :].to_broadcast([NP, 2, 1, IMGS]), ALU.mult).then_inc(sc_step, 1)
                        link(dve, v.tensor_tensor(scan2.unsqueeze(2), before, pt_[:, 1:3, ds(t, 1), :], ALU.mult),
                             sc_step, n + 2)
                        link(dve, v.tensor_tensor(ct_[:, :, ds(t, 1), :], scan1.unsqueeze(2), scan2[:, ::-1].unsqueeze(2), ALU.add),
                             sc_step, n + 3)
                v.tensor_scalar(mag[:, 0], cum[:, 0], 1e-10, None, ALU.max).then_inc(c_mx, 1)

                dve.wait_ge(c_inv, c + 1)
                link(dve, v.tensor_tensor(inv, mag[:, 0], mag[:, 1], ALU.mult), c_chain, l0 + 7)
                dve.wait_ge(c_inv, c + 1)
                link(dve, v.scalar_tensor_tensor(inv, inv, 2.0, mag[:, 1], ALU.subtract, ALU.mult), c_nw, c + 1)
                v.scalar_tensor_tensor(kT[par], inv, -1.0, kT[par], ALU.mult, ALU.mult).then_inc(c_qk, 1)
                v.tensor_tensor(qT[par], qT[par], cum[:, 0], ALU.mult).then_inc(c_qk, 1)

            dve.wait_ge(d_wo, 32)

            def out_stats(t, par, d=None):
                dve.wait_ge(o_mm, t + 3)
                link(dve, v.tensor_tensor(yst[par], PS[:, 4 + par, 0:D], bo, ALU.add), o_y, t + 3)
                v.bn_stats(bn6[par], yst[par]).then_inc(o_bn, 1)
                wait_apart(dve, o_bn, 2 * t + 1)
                link(dve, v.bn_aggr(stat[par][:, 0:2], bn6[par]), o_bn, 2 * t + 2)
                v.tensor_scalar(stat[par][:, 2:3], stat[par][:, 1:2], EPS, None, ALU.add).then_inc(o_ve, 1)

            def out_norm(t, par, d=None):
                dve.wait_ge(o_rs, t + 1)
                dve.wait_ge(o_hc, t + 1)
                dve.wait_ge(o_tr, t + 1)
                v.tensor_scalar(hn[par], yst[par], stat[par][:, 0:1], stat[par][:, 3:4], ALU.subtract, ALU.mult
                                ).then_inc(o_h, 1)

            staggered(dve, TT, out_stats, out_norm)

            for half in range(2):
                base = half * TT
                dve.wait_ge(m_dn, 2 + base)

                def dispatch(t, par, d=None):
                    n = t + base
                    lg = PS[:, 2 * par:2 * par + 2, :].rearrange("p b f -> p (b f)").rearrange("p (n s) -> p n s", s=SL)
                    ex = dl[par].rearrange("p (n s) -> p n s", s=SL)
                    dve.wait_ge(m_lg, n + 3)
                    link(dve, v.tensor_reduce(smx[:, 0:HE], lg, AX.X, ALU.max), m_max, n + 1)
                    dve.wait_ge(m_dn, n + 1)
                    v.tensor_tensor(ex, lg, smx[:, 0:HE].unsqueeze(2).to_broadcast([NP, HE, SL]), ALU.subtract
                                    ).then_inc(m_sub, 1)
                    dve.wait_ge(m_exp, n + 1)
                    link(dve, v.tensor_reduce(ssum[par], ex, AX.X, ALU.add), m_sum, n + 1)
                    v.reciprocal(ssum[par], ssum[par]).then_inc(m_rc, 1)

                tiles(dve, TT, dispatch)
                for b in range(4):
                    dve.wait_ge(m_x, 2 + base + TT)
                    v.tensor_scalar(xs[:, (half * 4 + b) * 2:(half * 4 + b) * 2 + 2].rearrange("p j d -> p (j d)"),
                                    PS[:, 4 + b, :], -33000.0, 65000.0, ALU.max, ALU.min).then_inc(x_cp, 1)

            dve.wait_ge(x_cp, 8)
            for j in range(SC):
                v.bn_stats(ebn[:, j], xs[:, j]).then_inc(e_bn, 1)
            dve.wait_ge(e_bn, SC)
            for j in range(SC):
                v.bn_aggr(est[:, j, 0:2], ebn[:, j]).then_inc(e_bn, 1)
            dve.wait_ge(e_bn, 2 * SC)
            v.tensor_scalar(est[:, :, 2], est[:, :, 1], EPS, None, ALU.add).then_inc(e_ve, 1)
            dve.wait_ge(e_rs, 1)
            v.scalar_tensor_tensor(est[:, :, 4], est[:, :, 0], -1.0, est[:, :, 3], ALU.mult, ALU.mult).then_inc(e_nb, 1)
            for j in range(SC):
                dve.wait_ge(e_mm, j + 3)
                v.tensor_copy(yt[:, j], PS[:, 2 + j % 2, 0:D]).then_inc(e_cp, 1)

            def combine_front(t, par, d=None):
                lg = PS[:, 0:4, :].rearrange("p b f -> p (b f)").rearrange("p (n s) -> p n s", s=SL)
                dve.wait_ge(f_lg, t + 3)
                link(dve, v.tensor_reduce(smx[:, 0:SL], lg.rearrange("p n s -> p s n"), AX.X, ALU.max), f_max, t + 1)
                dve.wait_ge(f_cn, 2 * t + 2)
                v.tensor_tensor(cl[par].rearrange("p (n s) -> p n s", s=SL), lg,
                                smx[:, 0:SL].unsqueeze(1).to_broadcast([NP, NE, SL]), ALU.subtract).then_inc(f_sub, 1)

            def combine_sum(t, par, d=None):
                dve.wait_ge(f_exp, t + 1)
                link(dve, v.tensor_reduce(ssum[par], cl[par].rearrange("p (n s) -> p s n", s=SL), AX.X, ALU.add),
                     f_sum, t + 1)
                v.reciprocal(ssum[par], ssum[par]).then_inc(f_rc, 1)

            def combine_stats(t, par, d=None):
                dve.wait_ge(f_y, t + 3)
                link(dve, v.tensor_tensor(yst[par].unsqueeze(1), PS[:, 6 + par:7 + par, 0:D], h1[:, ds(t, 1), :], ALU.add),
                     f_yb, t + 3)
                v.bn_stats(bn6[par], yst[par]).then_inc(f_bn, 1)
                wait_apart(dve, f_bn, 2 * t + 1)
                link(dve, v.bn_aggr(stat[par][:, 0:2], bn6[par]), f_bn, 2 * t + 2)
                v.tensor_scalar(stat[par][:, 2:3], stat[par][:, 1:2], EPS, None, ALU.add).then_inc(f_ve, 1)

            def combine_out(t, par, d):
                dve.wait_ge(f_rs, t + 1)
                dve.wait_ge(d_st[par], 16 * d + 16)
                v.tensor_scalar(hn[par], yst[par], stat[par][:, 0:1], stat[par][:, 3:4], ALU.subtract, ALU.mult
                                ).then_inc(f_o, 1)

            combine_front(0, 0)
            combine_sum(0, 0)
            with dve.Fori(0, TT // 2) as i:
                combine_front(2 * i + 1, 1)
                combine_stats(2 * i, 0)
                combine_sum(2 * i + 1, 1)
                combine_out(2 * i, 0, i)
                combine_front(2 * i + 2, 0)
                combine_stats(2 * i + 1, 1)
                combine_sum(2 * i + 2, 0)
                combine_out(2 * i + 1, 1, i)
            combine_stats(TT - 1, 0)
            combine_out(TT - 1, 0, TT // 2)

        @block.tensor
        def _(pe):
            t_ = nc.tensor
            pe.wait_ge(d_tokw, 16)
            pe.wait_ge(s_const, 9)
            for kc in range(KC):
                for e in range(KD):
                    ins = t_.transpose(PS[:, kc // 2, (kc % 2) * D + e * NP:(kc % 2) * D + (e + 1) * NP],
                                       tokW[:, e, kc * NP:(kc + 1) * NP], ident)
                if kc % 2:
                    ins.then_inc(wt_tr, 1)
            pe.wait_ge(pos_pre, 1)
            for k in range(KD):
                ins = t_.transpose(PS[:, 3, k * T:(k + 1) * T], pos_nat[0:T, k * NP:(k + 1) * NP], ident[0:T, 0:T])
            ins.then_inc(pos_tr, 1)
            pe.wait_ge(wt_cp, 3)
            pe.wait_ge(pos_cp, 1)

            def patches(q, par, d):
                for done in x_ord:
                    pe.wait_ge(done, 2 * q + 2)
                for u in range(2 * KC):
                    kc, half = u // 2, u % 2
                    pe.wait_ge(xt_act if u % 2 == 0 else xt_dve, 6 * q + u // 2 + 1)
                    for w in range(PH):
                        ins = t_.transpose(PS[:, u % 4, w * XP:(w + 1) * XP], xord[par][0:XP, kc, half * PH + w],
                                           ident[0:XP, 0:XP])
                    ins.then_inc(xt_tr, 1)
                pe.wait_ge(xt_act, 2 + 6 * q + 6)
                pe.wait_ge(xt_dve, 2 + 6 * q + 6)
                for j in range(4):
                    e, half = j // 2, j % 2
                    pe.wait_ge(h0_cp, 4 * q + j + 1)
                    for kc in range(KC):
                        ins = t_.matmul(PS[:, 4 + j, 0:PH * XP], tokWT[:, kc, e * NP:(e + 1) * NP],
                                        patchT[par][:, kc, half * PH:(half + 1) * PH, :].rearrange("p w r -> p (w r)"),
                                        start=kc == 0, stop=kc == KC - 1)
                    ins.then_inc(pt_mm, 1)

            tiles(pe, XQ, patches)

            def norm_sum(n, par, d=None):
                pe.wait_ge(n_sq, n + 1)
                pe.wait_ge(n_mx, n + 1)
                for k in range(KD):
                    ins = t_.matmul(PS[:, par, 0:PT], ones, nsq[par][:, k], start=k == 0, stop=k == KD - 1)
                ins.then_inc(n_mm, 1)

            tiles(pe, NPT, norm_sum)
            pe.wait_ge(n_xn, KD * NPT)
            pe.wait_ge(s_setup, 10)

            def project(c):
                par = c % 2
                pe.wait_ge(d_wc[par], 80 * (c // 2 + 1))
                with pe.Fori(0, NPT) as n:
                    u0 = (n + c * NPT) * 4
                    for tag in range(4):
                        pe.wait_ge(pj_cp, u0 + tag + 1)
                        for k in range(KD):
                            if tag < 2:
                                w = wc[par][:, k, 3:5, :].rearrange("p s n -> p (s n)")[:, tag::2]
                            else:
                                w = wc[par][:, k, tag - 2, :]
                            ins = t_.matmul(PS[:, tag, 0:PT], w, xnT[:, k, ds(n * PT, PT)], start=k == 0, stop=k == KD - 1)
                        ins.then_inc(pj_mm, 1)

            def attend(c):
                par_c = c % 2
                base = c * NG
                pe.wait_ge(c_qk, 2 * (c + 1))

                def front(gi, par, d=None):
                    n = gi + base
                    pe.wait_ge(a_st, 3 * n + 3)
                    pe.wait_ge(a_vcp, n + 1)
                    t_.matmul(PS[0:GT, 4, 0:NP], ones3[0:65, 0:GT], bias3[0:65, NS + c * NP:NS + (c + 1) * NP],
                              start=True, stop=False)
                    for k in range(KD):
                        ins = t_.matmul(PS[0:GT, 4, 0:NP], xst[par][:, k], wc[par_c][:, k, 2, :], start=False, stop=k == KD - 1)
                    ins.then_inc(a_v, 1)
                    pe.wait_ge(a_scp, n + 1)
                    for h in range(2):
                        rows = slice(h * DH, (h + 1) * DH)
                        ins = t_.matmul(PS[0:GT, 5 + h, 0:GT], kst[par][rows], qst[par][rows],
                                        start=True, stop=True)
                    ins.then_inc(a_s, 1)

                def back(gi, par, d=None):
                    n = gi + base
                    pe.wait_ge(a_vcp, n + 2)
                    pe.wait_ge(a_mk, 2 * n + 6)
                    pe.wait_ge(a_ocp, n + 1)
                    for h in range(2):
                        ins = t_.matmul(PS[h * DH:(h + 1) * DH, 7, 0:GT], vst[par][0:GT, h * DH:(h + 1) * DH],
                                        smk[par][0:GT, h], start=True, stop=True)
                    ins.then_inc(a_o, 1)

                staggered(pe, NG, front, back)

            project(0)
            for c in range(NC):
                if c + 1 < NC:
                    project(c + 1)
                attend(c)

            pe.wait_ge(d_phi, 16)
            for k in range(KD):
                for s in range(4):
                    if k:
                        pe.wait_ge(ph_cp, s + 1)
                    for b in range(4):
                        ins = t_.transpose(PS[:, s, b * NP:(b + 1) * NP], phi_nat[:, 4 * s + b, k * NP:(k + 1) * NP], ident)
                    ins.then_inc(ph_tr, 1)
            pe.wait_ge(d_wo, 32)

            def out_product(t, par, d):
                pe.wait_ge(d_ost[par], 32 * d + 32)
                pe.wait_ge(o_y, t + 1)
                pe.wait_ge(a_ocp, 1 + NC * NG)
                for k in range(KD):
                    t_.matmul(PS[:, 4 + par, k * NP:(k + 1) * NP], hst[par][:, k], ident, start=k == 0, stop=False,
                              skip_group_check=True)
                for c in range(NC):
                    ins = t_.matmul(PS[:, 4 + par, 0:D], ost[par][:, c], wo[:, c], start=False, stop=c == NC - 1,
                                    skip_group_check=True)
                ins.then_inc(o_mm, 1)

            def out_transpose(t, par, d=None):
                pe.wait_ge(o_h, t + 1)
                pe.wait_ge(o_tc, t + 1)
                for k in range(KD):
                    ins = t_.transpose(PS[:, 6 + par, k * NP:(k + 1) * NP], hn[par][:, k * NP:(k + 1) * NP], ident)
                ins.then_inc(o_tr, 1)

            out_product(0, 0, 0)
            with pe.Fori(0, TT // 2) as i:
                out_product(2 * i + 1, 1, i)
                out_transpose(2 * i, 0)
                out_product(2 * i + 2, 0, i + 1)
                out_transpose(2 * i + 1, 1)
            out_transpose(TT - 1, 0)

            def logits(bank, col, n_banks, par):
                for s in range(n_banks):
                    cols = slice(col + s * BANK, col + (s + 1) * BANK)
                    t_.matmul(PS[:, bank + s, :], ones3[0:65], bias3[0:65, cols], start=True, stop=False)
                    for k in range(KD):
                        ins = t_.matmul(PS[:, bank + s, :], hst[par][:, k], phiT[:, k, cols], start=False, stop=k == KD - 1)
                return ins

            pe.wait_ge(ph_cp, 8)
            pe.wait_ge(o_y, 2 + TT)
            pe.wait_ge(o_tc, 2 + TT)
            for half in range(2):
                base = half * TT
                if half:
                    pe.wait_ge(x_cp, 4)
                pe.wait_ge(m_sub, 2 + base)
                for b in range(4):
                    t_.matmul(PS[:, 4 + b, :], zeros3[0:1], bias3[0:1, 0:BANK], start=True, stop=False)

                def dispatch_logits(t, par, d):
                    n = t + base
                    pe.wait_ge(d_hst[par], 16 * (half * ((TT + 1) // 2 if par == 0 else TT // 2) + d + 1))
                    pe.wait_ge(m_sub, n + 1)
                    logits(2 * par, half * HS, 2, par).then_inc(m_lg, 1)

                def accumulate(t, par, last=False):
                    pe.wait_ge(m_dn, t + base + 3)
                    for j in range(SC // 2):
                        ins = t_.matmul(PS[:, 4 + j // 2, (j % 2) * D:(j % 2 + 1) * D], dn[par][:, j * NP:(j + 1) * NP],
                                        h1[:, t, :] if last else h1[:, ds(t, 1), :], start=False, stop=False,
                                        skip_group_check=True)
                    if last:
                        for b in range(4):
                            ins = t_.matmul(PS[:, 4 + b, :], zeros3[0:1], bias3[0:1, 0:BANK], start=False, stop=True)
                    ins.then_inc(m_x, 1)

                dispatch_logits(0, 0, 0)
                with pe.Fori(0, TT // 2) as i:
                    dispatch_logits(2 * i + 1, 1, i)
                    accumulate(2 * i, 0)
                    dispatch_logits(2 * i + 2, 0, i + 1)
                    accumulate(2 * i + 1, 1)
                accumulate(TT - 1, 0, last=True)

            pe.wait_ge(d_eb, 16)

            def transpose_slots(j):
                pe.wait_ge(e_th, j + 1)
                pe.wait_ge(e_tc, j + 1)
                for k in range(KD):
                    ins = t_.transpose(PS[:, j % 2, k * NP:(k + 1) * NP], xs[:, j, k * NP:(k + 1) * NP], ident)
                ins.then_inc(e_tr, 1)

            transpose_slots(0)
            for j in range(SC):
                if j + 1 < SC:
                    transpose_slots(j + 1)
                pe.wait_ge(e_tc, j + 3)
                pe.wait_ge(d_we[j % WEB], 32 * (j // WEB + 1))
                pe.wait_ge(e_cp, j + 1)
                bank = PS[:, 2 + j % 2, 0:D]
                for e in range(EC):
                    rows = slice(e * SL, (e + 1) * SL)
                    for k in range(KD):
                        t_.matmul(bank[rows], xtT[j % 2][:, k, rows], we[j % WEB][:, k, e], start=k == 0, stop=False,
                                  skip_group_check=True)
                t_.matmul(bank, chunk_sel[0:EC], eb[0:EC, j], start=False, stop=True, skip_group_check=True).then_inc(e_mm, 1)

            pe.wait_ge(e_cp, 2 + SC)
            hb = [2 * ((TT + 1) // 2), 2 * (TT // 2)]

            def combine_logits(t, par, d):
                pe.wait_ge(d_hst[par], 16 * (d + (hb[par] + 1)))
                pe.wait_ge(f_sub, t + 1)
                logits(0, 0, 4, par).then_inc(f_lg, 1)

            def combine(t, par, d=None):
                pe.wait_ge(f_cn, 2 * t + 6)

                def turn(b):
                    pe.wait_ge(f_tc, 4 * t + b + 1)
                    for j in range(4):
                        s = 4 * b + j
                        ins = t_.transpose(PS[:, 4 + b % 2, j * NP:(j + 1) * NP], cn[par][:, s * NP:(s + 1) * NP], ident)
                    ins.then_inc(f_tr, 1)

                def add(b):
                    if b == 0:
                        pe.wait_ge(f_yb, t + 1)
                    pe.wait_ge(f_tc, 4 * t + b + 3)
                    for j in range(4):
                        s = 4 * b + j
                        ins = t_.matmul(PS[:, 6 + par, 0:D], ct[par][:, s], yt[:, s], start=s == 0, stop=s == SC - 1)
                    return ins

                turn(0)
                turn(1)
                add(0)
                turn(2)
                add(1)
                turn(3)
                add(2)
                add(3).then_inc(f_y, 1)

            combine_logits(0, 0, 0)
            with pe.Fori(0, TT // 2) as i:
                combine_logits(2 * i + 1, 1, i)
                combine(2 * i, 0)
                combine_logits(2 * i + 2, 0, i + 1)
                combine(2 * i + 1, 1)
            combine(TT - 1, 0)


_INS = ['x', 'L0_tok_W', 'L0_tok_b', 'L0_tok_cls_token', 'L0_tok_pos_embed', 'L0_attn_gamma', 'L0_attn_W_qkv',
        'L0_attn_b_qkv', 'L0_attn_W_a', 'L0_attn_b_a', 'L0_attn_W_out', 'L0_attn_b_out', 'L0_ffn_phi_w',
        'L0_ffn_phi_b', 'L0_ffn_expert_w', 'L0_ffn_expert_b']


def kernel(**inputs):
    import numpy as _np
    import concourse.bacc as _bacc
    from concourse import mybir as _mybir
    from concourse.bass_utils import run_bass_kernel_spmd as _run

    nc = _bacc.Bacc("TRN2", target_bir_lowering=False, num_devices=1)
    arrays, args = {}, []
    for name in _INS:
        a = _np.ascontiguousarray(inputs[name])
        arrays[f"in_{name}_dram"] = a
        args.append(nc.dram_tensor(f"in_{name}_dram", a.shape, _mybir.dt.from_np(a.dtype), kind="ExternalInput").ap())
    n_img, n_tok, n_ch = inputs['x'].shape[0], inputs['L0_tok_pos_embed'].shape[1], inputs['L0_tok_W'].shape[0]
    args.append(nc.dram_tensor("out_0_dram", (n_img * n_tok, n_ch), _mybir.dt.float32, kind="ExternalOutput").ap())
    vit_tower_kernel(nc, *args)
    r = _run(nc, [arrays], core_ids=[0])
    return r.results[0]["out_0_dram"].reshape(n_img, n_tok, n_ch)
```

```python
import concourse.bass as bass
from concourse import mybir
from contextlib import ExitStack
import math


def vit_tower_kernel(nc, x, tok_w, tok_b, cls_token, pos_embed, gamma, w_qkv, b_qkv, w_a, b_a,
                     w_out, b_out, phi_w, phi_b, expert_w, expert_b, out):
    f32, bf16 = mybir.dt.float32, mybir.dt.bfloat16
    ALU, ACT, AX = mybir.AluOpType, mybir.ActivationFunctionType, mybir.AxisListType
    ds = bass.ds

    NP = 128
    BANK = 512
    IMGS, CIN, IMG, _ = x.shape
    D = tok_w.shape[0]
    T = pos_embed.shape[1]
    PATCH = 16
    SIDE = IMG // PATCH
    KD = D // NP
    TOK = IMGS * T
    KC = CIN * PATCH * PATCH // NP
    XQ = 4
    XB = IMGS // XQ
    XP = XB * SIDE
    PH = SIDE // 2
    INNER = w_out.shape[0]
    NC = INNER // NP
    DH = 64
    GI = 3
    GT = GI * T
    NG = -(-IMGS // GI)
    NPT = 6
    PT = 408
    TP = PT * NPT
    assert TP >= NG * GT and NG % 2 == 0
    NS = phi_w.shape[0]
    NE = expert_w.shape[0]
    SL = NS // NE
    SC = NS // NP
    EC = NP // SL
    HS = NS // 2
    HE = NE // 2
    TT = -(-TOK // NP)
    LASTR = TOK - (TT - 1) * NP
    assert TT % 2 == 1 and TP >= TT * NP
    EPS = 1e-5
    TINY = 2.0 ** -64
    NORM_SHIFT = 20

    ctx = ExitStack()
    with ctx:
        def sem(name):
            return ctx.enter_context(nc.semaphore(name))

        WORDS = 53200
        arena = ctx.enter_context(nc.sbuf_tensor("arena", [NP, WORDS], f32))
        PS = ctx.enter_context(nc.psum_tensor("PS", [NP, 8, BANK], f32))

        class Region:
            def __init__(self, start, end):
                self.at, self.end = start, end

            def take(self, *shape):
                n = math.prod(shape)
                a = arena[:, self.at:self.at + n]
                self.at += n
                assert self.at <= self.end, (self.at, self.end)
                if len(shape) == 1:
                    return a
                names = [f"d{i}" for i in range(len(shape))]
                return a.rearrange(f"p ({' '.join(names)}) -> p {' '.join(names)}",
                                   **{names[i]: shape[i] for i in range(1, len(shape))})

        keep = Region(0, WORDS)
        ident = keep.take(NP)
        ones = keep.take(NP)
        mask = keep.take(GT)
        gam = keep.take(KD)
        neghalf = keep.take(1)
        bias3 = keep.take((NS + INNER) // 2).bitcast(bf16)
        ones3 = keep.take(NP // 2).bitcast(bf16)
        zeros3 = keep.take(NP // 2).bitcast(bf16)
        wc = [keep.take(KD, 4, NP) for _ in range(2)]
        bc = [keep.take(5) for _ in range(2)]
        AB = 4
        qkst = [keep.take(2, GT) for _ in range(AB)]
        vst = [keep.take(NP) for _ in range(AB)]
        sraw = [keep.take(2, GT) for _ in range(2)]
        smk = [keep.take(2, GT) for _ in range(2)]
        stat = [keep.take(4) for _ in range(2)]
        bn6 = [keep.take(6) for _ in range(2)]
        terms = keep.take(2, 2, IMGS)
        h0T_at = keep.at
        h0T = keep.take(KD, TP)
        outT_at = keep.at
        outT = keep.take(NC, TP)
        xnT_at = keep.at
        xnT = keep.take(KD, TP)
        big_at = keep.at

        ra = Region(big_at, WORDS)
        xnat = [ra.take(CIN, PATCH, IMG) for _ in range(2)]
        patchT = [ra.take(KC, SIDE, XP) for _ in range(2)]
        tokW = ra.take(KD, KC * NP)
        tokWT = ra.take(KC, D)
        pos_nat = ra.take(D)
        posT = ra.take(KD, T)
        pos_add = ra.take(D)
        b3f = ra.take(NS + INNER)
        b3h = ra.take((NS + INNER) // 2).bitcast(bf16)
        xord = [Region(xnT_at, big_at).take(KC, SIDE, NP), Region(outT_at, xnT_at).take(KC, SIDE, NP)]
        rn = Region(outT_at, xnT_at)
        nsq = [rn.take(KD, PT) for _ in range(2)]
        nx = [rn.take(PT) for _ in range(2)]
        nl = [rn.take(PT) for _ in range(2)]
        nr = [rn.take(PT) for _ in range(2)]
        nt = [rn.take(PT) for _ in range(2)]
        vev = [rn.take(INNER) for _ in range(2)]
        xst = [rn.take(KD, GT) for _ in range(2)]
        wv = rn.take(KD, INNER)
        raw = h0T
        rb = Region(big_at, WORDS)
        pha = rb.take(3, TP)
        cum = rb.take(2, TP)
        mag = rb.take(2, TP)
        qk = [rb.take(2, TP) for _ in range(2)]
        inv = cum[:, 0]
        rc = Region(big_at, WORDS)
        phiT = rc.take(KD, NS)
        phi_nat = rc.take(SC, D)
        xs = phi_nat
        wo = rc.take(NC, D)
        bo = rc.take(D)
        h1 = rc.take(TT, D)
        h1T = rc.take(KD, TP)
        ost = [rc.take(NC, NP) for _ in range(2)]
        hst = [rc.take(KD, NP) for _ in range(2)]
        yst = [rc.take(D) for _ in range(2)]
        hn = [rc.take(D) for _ in range(2)]
        chunk_sel = rc.take(NP)
        smx = rc.take(NE)
        ssum = [rc.take(HE) for _ in range(2)]
        est = rc.take(SC, 5)
        ebn = rc.take(SC, 6)
        xtT = [rc.take(KD, NP) for _ in range(2)]
        rd = Region(xnT_at, big_at)
        dl = [rd.take(HS) for _ in range(2)]
        dn = [rd.take(HS) for _ in range(2)]
        yt = Region(xnT_at, big_at).take(SC, D)
        rf = Region(h0T_at, xnT_at)
        WEB = 5
        we = [rf.take(KD, EC, D) for _ in range(WEB)]
        eb = rf.take(SC, D)
        rg = Region(h0T_at, xnT_at)
        cl = [rg.take(NS) for _ in range(2)]
        cn = [rg.take(NS) for _ in range(2)]
        ct = [rg.take(SC, NP) for _ in range(2)]

        h0_dram = nc.dram_tensor("h0_scratch", (KD, NP, TP), f32, kind="Internal").ap()
        v_dram = nc.dram_tensor("v_scratch", (NG * GT, INNER), f32, kind="Internal").ap()
        qk_dram = nc.dram_tensor("qk_scratch", (NC, 2, NP, TP), f32, kind="Internal").ap()

        waited = sem("waited")
        d_tokw, d_pos, d_gam, d_b3 = sem("d_tokw"), sem("d_pos"), sem("d_gam"), sem("d_b3")
        d_x = [sem(f"d_x{i}") for i in range(2)]
        d_wc = [sem(f"d_wc{i}") for i in range(2)]
        d_wo, d_phi, d_eb = sem("d_wo"), sem("d_phi"), sem("d_eb")
        d_h0, d_wv = sem("d_h0"), sem("d_wv")
        d_v = [sem(f"d_v{i}") for i in range(2)]
        d_qk = [sem(f"d_qk{i}") for i in range(2)]
        d_grp = [sem(f"d_grp{i}") for i in range(AB)]
        v_st, v_mm, v_cp = sem("v_st"), sem("v_mm"), sem("v_cp")
        c_sq, c_ph = sem("c_sq"), sem("c_ph")
        d_ost = [sem(f"d_ost{i}") for i in range(2)]
        d_hst = [sem(f"d_hst{i}") for i in range(2)]
        d_we = [sem(f"d_we{i}") for i in range(WEB)]
        d_st = [sem(f"d_st{i}") for i in range(2)]
        s_const, s_pool, s_act, s_setup, s_pad = sem("s_const"), sem("s_pool"), sem("s_act"), sem("s_setup"), sem("s_pad")
        wt_tr, wt_cp, pos_pre, pos_tr, pos_cp = sem("wt_tr"), sem("wt_cp"), sem("pos_pre"), sem("pos_tr"), sem("pos_cp")
        x_ord = [sem(f"x_ord_{name}") for name in ("act", "dve", "pool")]
        xt_tr, xt_act, xt_dve = sem("xt_tr"), sem("xt_act"), sem("xt_dve")
        pt_mm, h0_cp, h0_cls = sem("pt_mm"), sem("h0_cp"), sem("h0_cls")
        n_sq, n_mm, n_mx, n_ln, n_rs, n_nw, n_xn = (sem(s) for s in ("n_sq", "n_mm", "n_mx", "n_ln", "n_rs", "n_nw", "n_xn"))
        pj_mm, pj_cp = sem("pj_mm"), sem("pj_cp")
        c_chain, c_m2, c_raw, c_lm, c_ex, c_ln, c_t, c_s, c_mx, c_il, c_inv, c_nw, c_qk = (
            sem(s) for s in ("c_chain", "c_m2", "c_raw", "c_lm", "c_ex", "c_ln", "c_t", "c_s", "c_mx", "c_il", "c_inv",
                             "c_nw", "c_qk"))
        sc_step = sem("sc_step")
        a_s, a_scp, a_mk, a_o, a_ocp = (sem(s) for s in ("a_s", "a_scp", "a_mk", "a_o", "a_ocp"))
        ph_tr, ph_cp = sem("ph_tr"), sem("ph_cp")
        o_mm, o_y, o_bn, o_ve, o_rs, o_h, o_hc, o_tr, o_tc = (
            sem(s) for s in ("o_mm", "o_y", "o_bn", "o_ve", "o_rs", "o_h", "o_hc", "o_tr", "o_tc"))
        m_lg, m_max, m_sub, m_exp, m_sum, m_rc, m_dn, m_x, x_cp = (
            sem(s) for s in ("m_lg", "m_max", "m_sub", "m_exp", "m_sum", "m_rc", "m_dn", "m_x", "x_cp"))
        e_bn, e_ve, e_rs, e_nb, e_th, e_tr, e_tc, e_mm, e_cp = (
            sem(s) for s in ("e_bn", "e_ve", "e_rs", "e_nb", "e_th", "e_tr", "e_tc", "e_mm", "e_cp"))
        f_lg, f_max, f_sub, f_exp, f_sum, f_rc, f_cn, f_tr, f_tc, f_y, f_yb, f_bn, f_ve, f_rs, f_o = (
            sem(s) for s in ("f_lg", "f_max", "f_sub", "f_exp", "f_sum", "f_rc", "f_cn", "f_tr", "f_tc", "f_y", "f_yb",
                             "f_bn", "f_ve", "f_rs", "f_o"))
        CREDITS = [(xt_tr, 24), (xt_act, 2), (xt_dve, 2), (pt_mm, 8), (h0_cp, 4), (n_mm, 2), (n_mx, 2), (pj_cp, 4),
                   (v_mm, 2), (v_cp, 2), (d_v[0], 16), (d_v[1], 16), (a_scp, 1), (a_mk, 2), (a_o, AB), (a_ocp, 2),
                   (o_mm, 2), (o_y, 2), (o_h, 2), (o_hc, 2), (o_tr, 2), (o_tc, 2),
                   (m_lg, 2), (m_sub, 2), (m_dn, 2), (m_x, 2), (e_tc, 2), (e_mm, 2), (e_cp, 2),
                   (f_lg, 2), (f_sub, 1), (f_cn, 4), (f_tr, 8), (f_tc, 2), (f_y, 2), (f_yb, 2),
                   (d_st[0], 16), (d_st[1], 16)]

        def wait_apart(eng, semaphore, value):
            eng.wait_ge(semaphore, value)
            eng.sem_inc(waited, 1)

        def link(eng, ins, semaphore, value):
            ins.then_inc(semaphore, 1)
            eng.wait_ge(semaphore, value)

        def staggered(eng, n, front, back):
            front(0, 0, 0)
            with eng.Fori(0, (n - 1) // 2) as i:
                front(2 * i + 1, 1, i)
                back(2 * i, 0, i)
                front(2 * i + 2, 0, i + 1)
                back(2 * i + 1, 1, i)
            if n % 2 == 0:
                front(n - 1, 1, n // 2 - 1)
                back(n - 2, 0, n // 2 - 1)
            back(n - 1, (n - 1) % 2, (n - 1) // 2)

        def by_fours(eng, body, first, last):
            with eng.Fori(first // AB, last // AB) as i:
                for u in range(AB):
                    body(AB * i + u, u, i)
            for u in range(last % AB):
                body(last - last % AB + u, u, last // AB)

        def staggered4(eng, n, front, back):
            front(0, 0, 0)
            with eng.Fori(0, (n - 1) // AB) as i:
                for u in range(AB):
                    front(AB * i + (u + 1), (u + 1) % AB, i + (u + 1) // AB)
                    back(AB * i + u, u, i)
            for t in range(AB * ((n - 1) // AB), n - 1):
                front(t + 1, (t + 1) % AB, (t + 1) // AB)
                back(t, t % AB, t // AB)
            back(n - 1, (n - 1) % AB, (n - 1) // AB)

        def tiles(eng, n, body):
            with eng.Fori(0, n // 2) as i:
                body(2 * i, 0, i)
                body(2 * i + 1, 1, i)
            if n % 2:
                body(n - 1, 0, n // 2)

        def by_token(a):
            return a[:, :, 0:TOK].rearrange("p r (b t) -> p r t b", t=T)

        def patch_order(eng, copy, q, par, d, who):
            eng.wait_ge(d_x[par], 16 * CIN * (d + 1))
            wait_apart(eng, xt_tr, q * (2 * KC) + 12)
            for kc in (2 * who, 2 * who + 1):
                src = xnat[par][0:XP, kc // 2, 8 * (kc % 2):8 * (kc % 2) + 8].rearrange("p i (w j) -> p w i j", j=PATCH)
                copy(xord[par][0:XP, kc].rearrange("p w (i j) -> p w i j", j=PATCH), src).then_inc(x_ord[who], 1)

        HALVES = [slice(0, IMGS // 2 * T), slice(IMGS // 2 * T, TP)]

        block = ctx.enter_context(nc.Block())

        @block.sync
        def _(sp):
            sp.dma_start(tokW, tok_w.rearrange("(e p) k -> p e k", p=NP)).then_inc(d_tokw, 16)
            sp.dma_start(pos_nat[0:T], pos_embed[0]).then_inc(d_pos, 16)
            sp.dma_start(pos_add[0:1], cls_token[0]).then_inc(d_pos, 16)
            sp.dma_start(pos_add[1:T], tok_b.rearrange("(a e) -> a e", a=1).to_broadcast([T - 1, D])).then_inc(d_pos, 16)
            xv = x.rearrange("b c (ph i) w -> b ph c (i w)", ph=SIDE)

            def load_x(q, par, d=None):
                for c in range(CIN):
                    sp.dma_start(xnat[par][0:XP, c].rearrange("p i w -> p (i w)"),
                                 xv[q * XB:(q + 1) * XB, :, c, :]).then_inc(d_x[par], 16)

            load_x(0, 0)
            load_x(1, 1)
            sp.dma_start(gam, gamma.rearrange("(k p) -> p k", p=NP), allow_slow_non_contiguous=True).then_inc(d_gam, 16)
            sp.wait_ge(s_const, 1)
            for r in range(3):
                sp.dma_start(b3f[32 * r:32 * r + 1, 0:NS], phi_b.rearrange("(a n) -> a n", a=1)).then_inc(d_b3, 16)
                sp.dma_start(b3f[32 * r:32 * r + 1, NS:NS + INNER],
                             b_qkv[2 * INNER:3 * INNER].rearrange("(a n) -> a n", a=1)).then_inc(d_b3, 16)

            def load_wc(c):
                par = c % 2
                for k in range(KD):
                    sp.dma_start(wc[par][:, k, 0:2, :],
                                 w_qkv[k * NP:(k + 1) * NP, :].rearrange("p (s n) -> p s n", s=3)[:, 0:2, c * NP:(c + 1) * NP]
                                 ).then_inc(d_wc[par], 16)
                sp.dma_start(wc[par][:, :, 2:4, :].rearrange("p k s n -> p k (s n)"),
                             w_a.rearrange("(k p) n -> p k n", p=NP)[:, :, c * 2 * NP:(c + 1) * 2 * NP]
                             ).then_inc(d_wc[par], 16)
                sp.dma_start(bc[par][:, 0:3], b_qkv.rearrange("(s c p) -> c p s", s=3, p=NP)[c], allow_slow_non_contiguous=True).then_inc(d_wc[par], 16)
                sp.dma_start(bc[par][:, 3:5], b_a.rearrange("(c p two) -> c p two", two=2, p=NP)[c], allow_slow_non_contiguous=True).then_inc(d_wc[par], 16)

            load_wc(0)
            load_wc(1)
            for q in range(2, XQ):
                for done in x_ord:
                    sp.wait_ge(done, 2 * (q - 1))
                load_x(q, q % 2)
            sp.wait_ge(h0_cp, 4 + 4 * XQ)
            sp.wait_ge(h0_cls, 1)
            sp.wait_ge(s_const, 9)
            for k in range(KD):
                sp.dma_start(h0_dram[k], h0T[:, k]).then_inc(d_h0, 16)
            sp.wait_ge(h0_cp, 4 + 4 * XQ)
            sp.dma_start(wv, w_qkv.rearrange("(k p) n -> p k n", p=NP)[:, :, 2 * INNER:3 * INNER]).then_inc(d_wv, 16)

            def store_v(n, par, d):
                sp.wait_ge(v_cp, n + 3)
                sp.dma_start(v_dram[ds(n * GT, GT), :], vev[par][0:GT]).then_inc(d_v[par], 16)

            tiles(sp, NG, store_v)
            for c in range(NC):
                if c + 2 < NC:
                    sp.wait_ge(pj_mm, 4 * NPT * (c + 1))
                    sp.wait_ge(pj_cp, 4 + 4 * NPT * (c + 1))
                    load_wc(c + 2)
                if c == 0:
                    sp.wait_ge(d_v[0], 16 + 16 * (NG // 2))
                    sp.wait_ge(d_v[1], 16 + 16 * (NG // 2))
                sp.wait_ge(d_qk[c % 2], 16 * (c // 2 + 1))
                sp.wait_ge(a_o, AB + c * NG)

                def load_group(gi, b, d):
                    sp.wait_ge(a_o, gi + (c * NG + 1))
                    sp.dma_start(qkst[b], qk_dram[c].rearrange("s p n -> p s n")[:, :, ds(gi * GT, GT)]
                                 ).then_inc(d_grp[b], 16)
                    sp.dma_start(vst[b][0:GT], v_dram[ds(gi * GT, GT), c * NP:(c + 1) * NP]).then_inc(d_grp[b], 16)

                by_fours(sp, load_group, 0, NG)
            sp.dma_start(phi_nat, phi_w.rearrange("(c p) d -> p c d", p=NP)).then_inc(d_phi, 16)
            sp.dma_start(wo, w_out.rearrange("(c p) d -> p c d", p=NP)).then_inc(d_wo, 16)
            sp.dma_start(bo, b_out.rearrange("(a n) -> a n", a=1).to_broadcast([NP, D])).then_inc(d_wo, 16)

            sp.wait_ge(a_ocp, 2 + NC * NG)

            def copy_out(t, par, d=None):
                sp.wait_ge(o_mm, t + 1)
                sp.dma_start(ost[par], outT[:, :, ds(t * NP, NP)]).then_inc(d_ost[par], 16)
                sp.dma_start(hst[par], h0_dram.rearrange("k p n -> p k n")[:, :, ds(t * NP, NP)]).then_inc(d_ost[par], 16)

            tiles(sp, TT, copy_out)

            sp.wait_ge(o_mm, 2 + TT)
            sp.wait_ge(s_pad, 1)

            def load_we(c):
                for k in range(KD):
                    sp.dma_start(we[c % WEB][:, k],
                                 expert_w[c * EC:(c + 1) * EC, k * NP:(k + 1) * NP, :].rearrange("e p h -> p e h")
                                 ).then_inc(d_we[c % WEB], 16)

            sp.wait_ge(d_ost[0], 32 * (TT // 2 + 1))
            sp.wait_ge(d_ost[1], 32 * (TT // 2))
            sp.dma_start(eb[0:EC], expert_b.rearrange("(c e) d -> e c d", e=EC)).then_inc(d_eb, 16)
            for half in range(2):
                base = half * TT
                sp.wait_ge(m_lg, 2 + base)

                def copy_h1(t, par, d=None):
                    if half == 0:
                        wait_apart(sp, o_tc, t + 3)
                    sp.wait_ge(m_lg, t + base + 1)
                    sp.dma_start(hst[par], h1T[:, :, ds(t * NP, NP)]).then_inc(d_hst[par], 16)

                tiles(sp, TT, copy_h1)
                for c in (range(WEB - 2), range(WEB - 2, WEB))[half]:
                    load_we(c)
            for c in range(WEB, SC):
                sp.wait_ge(e_mm, 2 + c - WEB + 1)
                load_we(c)
            sp.wait_ge(m_lg, 2 + 2 * TT)

            def copy_f(t, par, d=None):
                sp.wait_ge(f_lg, t + 1)
                sp.dma_start(hst[par], h1T[:, :, ds(t * NP, NP)]).then_inc(d_hst[par], 16)

            def store(t, par, rows=NP):
                sp.wait_ge(f_o, t + 1)
                sp.dma_start(out[ds(t * NP, rows), :], hn[par][0:rows]).then_inc(d_st[par], 16)

            copy_f(0, 0)
            copy_f(1, 1)
            with sp.Fori(0, TT // 2 - 1) as i:
                copy_f(2 * i + 2, 0)
                store(2 * i, 0)
                copy_f(2 * i + 3, 1)
                store(2 * i + 1, 1)
            copy_f(TT - 1, 0)
            store(TT - 3, 0)
            store(TT - 2, 1)
            store(TT - 1, 0, LASTR)
            sp.wait_ge(d_st[0], 16 + 16 * (TT // 2 + 1))
            sp.wait_ge(d_st[1], 16 + 16 * (TT // 2))

        @block.gpsimd
        def _(pool):
            g = nc.gpsimd
            for semaphore, n in CREDITS:
                pool.sem_inc(semaphore, n)
            g.memset(b3f, 0.0).then_inc(s_const, 1)
            g.memset(ident, 0.0).then_inc(s_pool, 1)
            g.memset(mask, float(DH) ** -0.5).then_inc(s_pool, 1)
            pool.wait_ge(s_pool, 2)
            g.affine_select(out=ident, in_=ident, compare_op=ALU.not_equal, fill=1.0, base=0,
                            pattern=[[-1, NP]], channel_multiplier=1).then_inc(s_const, 1)
            g.memset(bias3, 0.0).then_inc(s_const, 1)
            g.memset(ones3, 1.0).then_inc(s_const, 1)
            g.memset(zeros3, 0.0).then_inc(s_const, 1)
            g.memset(ones, 1.0).then_inc(s_const, 1)
            g.memset(neghalf, -0.5).then_inc(s_const, 1)
            for k in range(KD):
                g.memset(h0T[:, k, TOK:TP], 0.0).then_inc(s_const, 1)
            g.affine_select(out=mask, in_=mask, compare_op=ALU.is_ge, fill=0.0, base=0,
                            pattern=[[1, GT]], channel_multiplier=-1).then_inc(s_pool, 1)
            pool.wait_ge(s_pool, 3)
            m3 = mask.rearrange("p (b t) -> p b t", t=T)
            g.affine_select(out=m3, in_=m3, compare_op=ALU.is_ge, fill=0.0, base=0,
                            pattern=[[-T, GI], [0, T]], channel_multiplier=1).then_inc(s_pool, 1)
            pool.wait_ge(s_pool, 4)

            tiles(pool, XQ, lambda q, par, d: patch_order(pool, g.tensor_copy, q, par, d, 2))

            pool.wait_ge(n_xn, KD * NPT)

            def stage(n, par, d):
                pool.wait_ge(v_mm, n + 1)
                g.tensor_copy(xst[par], xnT[:, :, ds(n * GT, GT)]).then_inc(v_st, 1)

            tiles(pool, NG, stage)

            def apply_masks(c):
                base = c * NG

                def apply_mask(gi, b, d):
                    par = b % 2
                    n = gi + base
                    pool.wait_ge(a_scp, n + 2)
                    pool.wait_ge(a_o, n + 3)
                    g.tensor_tensor(smk[par][0:GT], sraw[par][0:GT], mask[0:GT].unsqueeze(1).to_broadcast([GT, 2, GT]),
                                    ALU.mult).then_inc(a_mk, 1)

                by_fours(pool, apply_mask, 0, NG)

            for c in range(NC):
                if c:
                    apply_masks(c - 1)
                pool.wait_ge(c_qk, 3 * (c + 1))
                pool.dma_start(qk_dram[c].rearrange("s p n -> p s n"), qk[c % 2]).then_inc(d_qk[c % 2], 16)
            apply_masks(NC - 1)

            pool.wait_ge(a_ocp, 2 + NC * NG)
            g.memset(h1[LASTR:NP, TT - 1], 0.0).then_inc(s_pool, 1)
            pool.wait_ge(s_pool, 5)
            g.memset(h1T[:, :, TOK:TP], 0.0).then_inc(s_pool, 1)
            g.memset(chunk_sel, 1.0).then_inc(s_pool, 1)
            pool.wait_ge(s_pool, 7)
            sel3 = chunk_sel.rearrange("p (e s) -> p e s", s=SL)
            g.affine_select(out=sel3, in_=sel3, compare_op=ALU.is_equal, fill=0.0, base=0,
                            pattern=[[-1, EC], [0, SL]], channel_multiplier=1).then_inc(s_pool, 1)
            pool.wait_ge(s_pool, 8)
            pool.sem_inc(s_pad, 1)

            def out_rstd(t, par, d=None):
                pool.wait_ge(o_ve, t + 1)
                g.tensor_tensor(stat[par][:, 3:4], stat[par][:, 2:3], neghalf, ALU.pow).then_inc(o_rs, 1)

            tiles(pool, TT, out_rstd)

            for half in range(2):
                base = half * TT
                pool.wait_ge(m_x, 2 + base)

                def normalise(t, par, d=None):
                    n = t + base
                    pool.wait_ge(m_rc, n + 1)
                    pool.wait_ge(m_x, n + 1)
                    g.tensor_tensor(dn[par].rearrange("p (n s) -> p n s", s=SL),
                                    dl[par].rearrange("p (n s) -> p n s", s=SL),
                                    ssum[par].unsqueeze(2).to_broadcast([NP, HE, SL]),
                                    ALU.mult).then_inc(m_dn, 1)

                tiles(pool, TT, normalise)

            pool.wait_ge(e_ve, 1)
            g.tensor_tensor(est[:, :, 3], est[:, :, 2], neghalf.to_broadcast([NP, SC]), ALU.pow).then_inc(e_rs, 1)

            pool.wait_ge(e_mm, 2 + SC)

            def combine_norm(t, par, d=None):
                pool.wait_ge(f_rc, t + 1)
                pool.wait_ge(f_tr, 4 * t + 4)
                for h in range(2):
                    part = slice(h * HS, (h + 1) * HS)
                    g.tensor_tensor(cn[par][:, part].rearrange("p (n s) -> p n s", s=SL),
                                    cl[par][:, part].rearrange("p (n s) -> p n s", s=SL),
                                    ssum[par].unsqueeze(1).to_broadcast([NP, HE, SL]),
                                    ALU.mult).then_inc(f_cn, 1)

            def combine_rstd(t, par, d=None):
                pool.wait_ge(f_ve, t + 1)
                g.tensor_tensor(stat[par][:, 3:4], stat[par][:, 2:3], neghalf, ALU.pow).then_inc(f_rs, 1)

            combine_norm(0, 0)
            with pool.Fori(0, TT // 2) as i:
                combine_rstd(2 * i, 0)
                combine_norm(2 * i + 1, 1)
                combine_rstd(2 * i + 1, 1)
                combine_norm(2 * i + 2, 0)
            combine_rstd(TT - 1, 0)

        @block.scalar
        def _(act):
            a = nc.scalar
            for j in range(3):
                act.wait_ge(wt_tr, j + 1)
                a.activation(tokWT[:, 2 * j:2 * j + 2, :].rearrange("p k e -> p (k e)"), PS[:, j, :], ACT.Copy
                             ).then_inc(wt_cp, 1)

            def patch_copies(q, par, d=None):
                act.wait_ge(pt_mm, 4 * q + 4)
                for u in range(0, 2 * KC, 2):
                    act.wait_ge(xt_tr, q * (2 * KC) + u + 25)
                    a.activation(patchT[par][:, u // 2, 0:PH, :].rearrange("p w r -> p (w r)"),
                                 PS[:, u % 4, 0:PH * XP], ACT.Copy).then_inc(xt_act, 1)

            def copy_act(dst, src):
                return a.activation(dst, src, ACT.Copy)

            staggered(act, XQ, lambda q, par, d: patch_order(act, copy_act, q, par, d, 0), patch_copies)

            act.wait_ge(h0_cp, 4 + 4 * XQ)
            act.wait_ge(h0_cls, 1)
            act.wait_ge(s_const, 9)

            def norm_square(n, par, d=None):
                act.wait_ge(n_mm, n + 1)
                a.activation(nsq[par], h0T[:, :, ds(n * PT, PT)], ACT.Square).then_inc(n_sq, 1)

            def norm_rsqrt(n, par, d=None):
                act.wait_ge(n_mx, n + 3)
                a.activation(nl[par], nx[par], ACT.Ln, scale=2.0 ** NORM_SHIFT).then_inc(n_ln, 1)
                act.wait_ge(n_ln, n + 1)
                a.activation(nr[par], nl[par], ACT.Exp, scale=-0.5, bias=0.5 * NORM_SHIFT * math.log(2.0)
                             ).then_inc(n_rs, 1)

            staggered(act, NPT, norm_square, norm_rsqrt)

            def project_copies(c):
                par = c % 2
                act.wait_ge(d_wc[par], 80 * (c // 2 + 1))
                if c == 0:
                    act.wait_ge(n_xn, KD * NPT)
                    act.wait_ge(d_h0, 16 * KD)
                else:
                    act.wait_ge(c_ph, 4 * c)
                if c >= 2:
                    act.wait_ge(d_qk[par], 16 * (c // 2))
                with act.Fori(0, NPT) as n:
                    cols = ds(n * PT, PT)
                    u0 = (n + c * NPT) * 4
                    for tag, (dst, b) in enumerate(((raw[:, 0, cols], 3), (raw[:, 1, cols], 4),
                                                    (qk[par][:, 0, cols], 0), (qk[par][:, 1, cols], 1))):
                        act.wait_ge(pj_mm, u0 + tag + 1)
                        a.activation(dst, PS[:, tag, 0:PT], ACT.Identity, bias=bc[par][:, b:b + 1]).then_inc(pj_cp, 1)

            def attend_front(c, gi, b):
                n = gi + c * NG
                act.wait_ge(a_s, n + 1)
                act.wait_ge(a_mk, n + 1)
                a.activation(sraw[b % 2][0:GT], PS[0:GT, 4:6, 0:GT], ACT.Copy).then_inc(a_scp, 1)

            def attend_back(c, gi, b):
                act.wait_ge(a_o, gi + (c * NG + AB + 1))
                a.activation(outT[:, c, ds(gi * GT, GT)], PS[:, 6 + b % 2, 0:GT], ACT.Copy).then_inc(a_ocp, 1)

            BETWEEN = [9, 10, 11, 12, 13, 15, 17, 19, 21, NG]

            def attend_start(c):
                attend_front(c, 0, 0)
                with act.Fori(0, BETWEEN[0] // AB) as i:
                    for u in range(AB):
                        attend_front(c, AB * i + (u + 1), (u + 1) % AB)
                        attend_back(c, AB * i + u, u)

            def values(n, par, d):
                act.wait_ge(v_mm, n + 3)
                act.wait_ge(d_v[par], 16 * d + 16)
                a.activation(vev[par][0:GT], PS[0:GT, 4 + par, :], ACT.Copy).then_inc(v_cp, 1)

            VALUES = [0, 1, 2, 4, 6, 8, 10, 12]

            def attend_between(c, step):
                if c == -2:
                    for n in range(VALUES[step - 3], VALUES[step - 2]):
                        values(n, n % 2, n // 2)
                if c < 0:
                    return
                for gi in range(BETWEEN[step - 1], BETWEEN[step]):
                    attend_front(c, gi, gi % AB)
                    attend_back(c, gi - 1, (gi - 1) % AB)
                if step == len(BETWEEN) - 1:
                    attend_back(c, NG - 1, (NG - 1) % AB)

            def phasor_scale(c):
                act.wait_ge(pj_cp, 4 + 4 * NPT * (c + 1))
                if c:
                    act.wait_ge(c_qk, 3 * c)
                for h, cols in enumerate(HALVES):
                    for part in range(2):
                        a.activation(mag[:, part, cols], raw[:, part, cols], ACT.Square).then_inc(c_sq, 1)
                    attend_between(c - 2, 3 + h)
                for h, cols in enumerate(HALVES):
                    act.wait_ge(c_m2, 2 * c + h + 1)
                    act.wait_ge(c_raw, 2 * c + h + 1)
                    a.activation(mag[:, 0, cols], mag[:, 0, cols], ACT.Ln).then_inc(c_lm, 1)
                attend_between(c - 2, 5)
                for h, cols in enumerate(HALVES):
                    act.wait_ge(c_lm, 2 * c + h + 1)
                    a.activation(mag[:, 1, cols], mag[:, 0, cols], ACT.Exp, scale=0.5).then_inc(c_ex, 1)
                attend_between(c - 2, 6)
                for h, cols in enumerate(HALVES):
                    act.wait_ge(c_ex, 4 * c + h + 1)
                    a.activation(mag[:, 1, cols], mag[:, 1, cols], ACT.Exp, scale=-1.0).then_inc(c_ex, 1)
                attend_between(c - 2, 7)
                for h, cols in enumerate(HALVES):
                    act.wait_ge(c_ex, 4 * c + h + 3)
                    a.activation(mag[:, 1, cols], mag[:, 1, cols], ACT.Ln, bias=1.0).then_inc(c_ln, 1)
                attend_between(c - 2, 8)
                for h, cols in enumerate(HALVES):
                    act.wait_ge(c_t, 2 * c + h + 1)
                    a.activation(mag[:, 0, cols], mag[:, 0, cols], ACT.Exp, scale=-1.0).then_inc(c_s, 1)
                attend_between(c - 2, 9)

            def inverse(c):
                for h, cols in enumerate(HALVES):
                    act.wait_ge(c_mx, 2 * c + h + 1)
                    a.activation(mag[:, 1, cols], mag[:, 0, cols], ACT.Ln).then_inc(c_il, 1)
                attend_between(c - 1, 1)
                for h, cols in enumerate(HALVES):
                    act.wait_ge(c_il, 2 * c + h + 1)
                    a.activation(mag[:, 1, cols], mag[:, 1, cols], ACT.Exp, scale=-1.0).then_inc(c_inv, 1)
                attend_between(c - 1, 2)

            project_copies(0)
            for c in range(NC):
                phasor_scale(c)
                if c == 0:
                    with act.Fori(VALUES[-1] // 2, NG // 2) as i:
                        values(2 * i, 0, i)
                        values(2 * i + 1, 1, i)
                if c + 1 < NC:
                    project_copies(c + 1)
                if c:
                    attend_start(c - 1)
                inverse(c)
            for step in range(3, len(BETWEEN)):
                attend_between(NC - 2, step)
            staggered4(act, NG, lambda gi, b, d: attend_front(NC - 1, gi, b), lambda gi, b, d: attend_back(NC - 1, gi, b))

            for j in range(2 * KD * 2):
                act.wait_ge(ph_tr, j + 1)
                k, s = j // 4, j % 4
                a.activation(phiT[:, k, s * BANK:(s + 1) * BANK], PS[:, s, :], ACT.Copy).then_inc(ph_cp, 1)

            def keep_h1(t, par, rows=NP):
                act.wait_ge(o_h, t + 3)
                a.activation(h1[0:rows, ds(t, 1), :], hn[par][0:rows].unsqueeze(1), ACT.Copy).then_inc(o_hc, 1)
                act.wait_ge(o_tr, t + 3)
                a.activation(h1T[:, :, ds(t * NP, rows)],
                             PS[:, 6 + par, 0:D].rearrange("p (k n) -> p k n", k=KD)[:, :, 0:rows], ACT.Copy
                             ).then_inc(o_tc, 1)

            act.wait_ge(s_pad, 1)
            with act.Fori(0, TT // 2) as i:
                keep_h1(2 * i, 0)
                keep_h1(2 * i + 1, 1)
            keep_h1(TT - 1, 0, LASTR)

            for half in range(2):
                def dispatch_exp(t, par, d=None):
                    act.wait_ge(m_sub, t + half * TT + 3)
                    a.activation(dl[par], dl[par], ACT.Exp).then_inc(m_exp, 1)

                tiles(act, TT, dispatch_exp)

            act.wait_ge(e_nb, 1)
            for j in range(SC):
                a.activation(xs[:, j], xs[:, j], ACT.Tanh, bias=est[:, j, 4:5], scale=est[:, j, 3:4]).then_inc(e_th, 1)
            for j in range(SC):
                act.wait_ge(e_tr, j + 1)
                act.wait_ge(e_mm, j + 1)
                a.activation(xtT[j % 2], PS[:, j % 2, 0:D].rearrange("p (k n) -> p k n", k=KD), ACT.Copy).then_inc(e_tc, 1)

            def combine_exp(t, par, d=None):
                act.wait_ge(f_sub, t + 2)
                a.activation(cl[par], cl[par], ACT.Exp).then_inc(f_exp, 1)

            def combine_copies(t, par, d=None):
                act.wait_ge(f_y, t + 1)
                for b in range(4):
                    act.wait_ge(f_tr, 4 * t + b + 9)
                    a.activation(ct[par][:, 4 * b:4 * b + 4, :],
                                 PS[:, 4 + b % 2, :].rearrange("p (j n) -> p j n", n=NP), ACT.Copy).then_inc(f_tc, 1)

            act.wait_ge(e_mm, 2 + SC)
            combine_exp(0, 0)
            with act.Fori(0, TT // 2) as i:
                combine_copies(2 * i, 0)
                combine_exp(2 * i + 1, 1)
                combine_copies(2 * i + 1, 1)
                combine_exp(2 * i + 2, 0)
            combine_copies(TT - 1, 0)

        @block.vector
        def _(dve):
            v = nc.vector
            dve.wait_ge(d_pos, 48)
            v.tensor_tensor(pos_nat[0:T], pos_nat[0:T], pos_add[0:T], ALU.add).then_inc(pos_pre, 1)
            dve.wait_ge(d_gam, 16)
            link(dve, v.tensor_scalar(gam, gam, math.sqrt(D), None, ALU.mult), s_setup, 1)
            dve.wait_ge(pos_tr, 1)
            v.tensor_copy(posT.rearrange("p k t -> p (k t)"), PS[:, 3, 0:KD * T]).then_inc(pos_cp, 1)
            dve.wait_ge(pos_cp, 1)

            def patch_copies(q, par, d=None):
                dve.wait_ge(pt_mm, 4 * q + 4)
                for u in range(1, 2 * KC, 2):
                    dve.wait_ge(xt_tr, q * (2 * KC) + u + 25)
                    v.tensor_copy(patchT[par][:, u // 2, PH:SIDE, :].rearrange("p w r -> p (w r)"),
                                  PS[:, u % 4, 0:PH * XP]).then_inc(xt_dve, 1)
                for j in range(4):
                    e, half = j // 2, j % 2
                    dve.wait_ge(pt_mm, 8 + 4 * q + j + 1)
                    src = PS[:, 4 + j, 0:PH * XP].rearrange("p (w b s) -> p s b w", w=PH, b=XB)
                    dst = h0T[:, e, ds(q * (XB * T), XB * T)].rearrange("p (b t) -> p b t", t=T)[:, :, 1:T] \
                        .rearrange("p b (s w) -> p s b w", s=SIDE)
                    add = posT[:, e, 1:T].rearrange("p (s w) -> p s w", s=SIDE)
                    for s in range(SIDE):
                        ins = v.tensor_tensor(dst[:, s, :, half * PH:(half + 1) * PH], src[:, s],
                                              add[:, s, half * PH:(half + 1) * PH].unsqueeze(1).to_broadcast([NP, XB, PH]),
                                              ALU.add)
                    ins.then_inc(h0_cp, 1)

            staggered(dve, XQ, lambda q, par, d: patch_order(dve, v.tensor_copy, q, par, d, 1), patch_copies)
            v.tensor_copy(h0T[:, :, 0:TOK].rearrange("p k (b t) -> p k b t", t=T)[:, :, :, 0],
                          posT[:, :, 0:1].to_broadcast([NP, KD, IMGS])).then_inc(h0_cls, 1)

            nb = NS + INNER
            dve.wait_ge(d_b3, 96)
            dve.wait_ge(s_const, 9)
            for r in range(3):
                row = slice(32 * r, 32 * r + 1)
                link(dve, v.tensor_copy(b3h[0:65, 0:nb], b3f[0:65]), s_setup, 2 + 3 * r)
                link(dve, v.tensor_copy(bias3[row, 0:nb], b3h[row, 0:nb]), s_setup, 3 + 3 * r)
                link(dve, v.tensor_tensor(b3f[0:65], b3f[0:65], b3h[0:65, 0:nb], ALU.subtract), s_setup, 4 + 3 * r)

            dve.wait_ge(h0_cls, 1)

            def norm_max(n, par, d=None):
                dve.wait_ge(n_mm, n + 3)
                v.tensor_scalar(nx[par], PS[:, par, 0:PT], 1e-24, None, ALU.max).then_inc(n_mx, 1)

            def norm_apply(n, par, d=None):
                dve.wait_ge(n_rs, n + 1)
                link(dve, v.tensor_tensor(nt[par], nr[par], nr[par], ALU.mult), n_nw, 3 * n + 1)
                link(dve, v.scalar_tensor_tensor(nt[par], nt[par], -0.5, nx[par], ALU.mult, ALU.mult), n_nw, 3 * n + 2)
                link(dve, v.scalar_tensor_tensor(nr[par], nt[par], 1.5, nr[par], ALU.add, ALU.mult), n_nw, 3 * n + 3)
                for k in range(KD):
                    v.scalar_tensor_tensor(xnT[:, k, ds(n * PT, PT)], h0T[:, k, ds(n * PT, PT)], gam[:, k:k + 1],
                                           nr[par], ALU.mult, ALU.mult).then_inc(n_xn, 1)

            staggered(dve, NPT, norm_max, norm_apply)

            dve.wait_ge(n_xn, KD * NPT)
            v.memset(cum[:, :, TOK:TP], 0.0).then_inc(s_setup, 1)
            dve.wait_ge(s_setup, 11)
            ct_ = by_token(cum)
            pt_ = by_token(pha)
            turn = bass.AP(tensor=pha.tensor, offset=pha.offset, ap=[pha.ap[0], (TP, 2), (TP, 2), (1, TOK)]
                           ).rearrange("p g j (b t) -> p g j t b", t=T)

            for c in range(NC):
                par = c % 2
                dve.wait_ge(pj_cp, 4 + 4 * NPT * (c + 1))
                for h, cols in enumerate(HALVES):
                    l0 = 3 * (2 * c + h)
                    dve.wait_ge(c_sq, 4 * c + 2 * h + 2)
                    link(dve, v.tensor_tensor(mag[:, 0, cols], mag[:, 0, cols], mag[:, 1, cols], ALU.add), c_chain, l0 + 1)
                    link(dve, v.tensor_scalar(mag[:, 1, cols], mag[:, 0, cols], TINY, math.sqrt(TINY), ALU.is_lt, ALU.mult),
                         c_chain, l0 + 2)
                    v.tensor_scalar(mag[:, 0, cols], mag[:, 0, cols], TINY, None, ALU.max).then_inc(c_m2, 1)
                    link(dve, v.tensor_tensor(raw[:, 0, cols], raw[:, 0, cols], mag[:, 1, cols], ALU.add), c_chain, l0 + 3)
                    dve.sem_inc(c_raw, 1)
                for h, cols in enumerate(HALVES):
                    dve.wait_ge(c_ln, 2 * c + h + 1)
                    v.scalar_tensor_tensor(mag[:, 0, cols], mag[:, 0, cols], 0.5, mag[:, 1, cols], ALU.mult, ALU.add
                                           ).then_inc(c_t, 1)
                for h, cols in enumerate(HALVES):
                    dve.wait_ge(c_s, 2 * c + h + 1)
                    v.scalar_tensor_tensor(pha[:, 0, cols], raw[:, 1, cols], -1.0, mag[:, 0, cols], ALU.mult, ALU.mult
                                           ).then_inc(c_ph, 1)
                    v.tensor_tensor(pha[:, 1:3, cols], raw[:, :, cols],
                                    mag[:, 0:1, cols].to_broadcast([NP, 2, cols.stop - cols.start]), ALU.mult).then_inc(c_ph, 1)
                dve.wait_ge(c_ph, 4 * (c + 1))

                s0 = c * (1 + 2 * (T - 1))
                link(dve, v.tensor_copy(ct_[:, :, 0, :], pt_[:, 1:3, 0, :][:, ::-1]), sc_step, s0 + 1)
                UN = 4
                with dve.Fori(0, (T - 1) // UN) as i:
                    for u in range(UN):
                        t = i * UN + (u + 1)
                        n = s0 + 1 + 2 * (i * UN + u)
                        before = ct_[:, :, ds(i * UN + u, 1), :].rearrange("p j o b -> p o j b").to_broadcast([NP, 2, 2, IMGS])
                        by = turn[:, :, :, ds(t, 1), :].rearrange("p g j o b -> p g j (o b)")
                        link(dve, v.tensor_tensor(terms, before, by, ALU.mult), sc_step, n + 1)
                        link(dve, v.tensor_tensor(ct_[:, :, ds(t, 1), :], terms[:, ::-1, 0].unsqueeze(2),
                                                  terms[:, ::-1, 1].unsqueeze(2), ALU.add), sc_step, n + 2)
                for cols in HALVES:
                    v.tensor_scalar(mag[:, 0, cols], cum[:, 1, cols], 1e-10, None, ALU.max).then_inc(c_mx, 1)

                v.tensor_tensor(qk[par][:, 0], qk[par][:, 0], cum[:, 1], ALU.mult).then_inc(c_qk, 1)
                for h, cols in enumerate(HALVES):
                    dve.wait_ge(c_inv, 2 * c + h + 1)
                    link(dve, v.tensor_tensor(inv[:, cols], mag[:, 0, cols], mag[:, 1, cols], ALU.mult), c_nw, 4 * c + 2 * h + 1)
                    link(dve, v.scalar_tensor_tensor(inv[:, cols], inv[:, cols], 2.0, mag[:, 1, cols], ALU.subtract, ALU.mult),
                         c_nw, 4 * c + 2 * h + 2)
                    v.scalar_tensor_tensor(qk[par][:, 1, cols], inv[:, cols], -1.0, qk[par][:, 1, cols], ALU.mult, ALU.mult
                                           ).then_inc(c_qk, 1)

            dve.wait_ge(d_wo, 32)

            def out_stats(t, par, d=None):
                dve.wait_ge(o_h, t + 1)
                dve.wait_ge(o_mm, t + 3)
                link(dve, v.tensor_tensor(yst[par], PS[:, 4 + par, 0:D], bo, ALU.add), o_y, t + 3)
                v.bn_stats(bn6[par], yst[par]).then_inc(o_bn, 1)
                wait_apart(dve, o_bn, 2 * t + 1)
                link(dve, v.bn_aggr(stat[par][:, 0:2], bn6[par]), o_bn, 2 * t + 2)
                v.tensor_scalar(stat[par][:, 2:3], stat[par][:, 1:2], EPS, None, ALU.add).then_inc(o_ve, 1)

            def out_norm(t, par, d=None):
                dve.wait_ge(o_rs, t + 1)
                dve.wait_ge(o_hc, t + 1)
                dve.wait_ge(o_tr, t + 1)
                v.tensor_scalar(hn[par], yst[par], stat[par][:, 0:1], stat[par][:, 3:4], ALU.subtract, ALU.mult
                                ).then_inc(o_h, 1)

            staggered(dve, TT, out_stats, out_norm)

            for half in range(2):
                base = half * TT
                dve.wait_ge(m_dn, 2 + base)

                def dispatch(t, par, d=None):
                    n = t + base
                    lg = PS[:, 2 * par:2 * par + 2, :].rearrange("p b f -> p (b f)").rearrange("p (n s) -> p n s", s=SL)
                    ex = dl[par].rearrange("p (n s) -> p n s", s=SL)
                    dve.wait_ge(m_lg, n + 3)
                    link(dve, v.tensor_reduce(smx[:, 0:HE], lg, AX.X, ALU.max), m_max, n + 1)
                    dve.wait_ge(m_dn, n + 1)
                    v.tensor_tensor(ex, lg, smx[:, 0:HE].unsqueeze(2).to_broadcast([NP, HE, SL]), ALU.subtract
                                    ).then_inc(m_sub, 1)
                    dve.wait_ge(m_exp, n + 1)
                    link(dve, v.tensor_reduce(ssum[par], ex, AX.X, ALU.add), m_sum, n + 1)
                    v.reciprocal(ssum[par], ssum[par]).then_inc(m_rc, 1)

                tiles(dve, TT, dispatch)
                for b in range(4):
                    dve.wait_ge(m_x, 2 + base + TT)
                    v.tensor_scalar(xs[:, (half * 4 + b) * 2:(half * 4 + b) * 2 + 2].rearrange("p j d -> p (j d)"),
                                    PS[:, 4 + b, :], -33000.0, 65000.0, ALU.max, ALU.min).then_inc(x_cp, 1)

            dve.wait_ge(x_cp, 8)
            for j in range(SC):
                v.bn_stats(ebn[:, j], xs[:, j]).then_inc(e_bn, 1)
            dve.wait_ge(e_bn, SC)
            for j in range(SC):
                v.bn_aggr(est[:, j, 0:2], ebn[:, j]).then_inc(e_bn, 1)
            dve.wait_ge(e_bn, 2 * SC)
            v.tensor_scalar(est[:, :, 2], est[:, :, 1], EPS, None, ALU.add).then_inc(e_ve, 1)
            dve.wait_ge(e_rs, 1)
            v.scalar_tensor_tensor(est[:, :, 4], est[:, :, 0], -1.0, est[:, :, 3], ALU.mult, ALU.mult).then_inc(e_nb, 1)
            for j in range(SC):
                dve.wait_ge(e_mm, j + 3)
                v.tensor_copy(yt[:, j], PS[:, 2 + j % 2, 0:D]).then_inc(e_cp, 1)

            def combine_front(t, par, d=None):
                lg = PS[:, 0:4, :].rearrange("p b f -> p (b f)").rearrange("p (n s) -> p n s", s=SL)
                dve.wait_ge(f_lg, t + 3)
                link(dve, v.tensor_reduce(smx[:, 0:SL], lg.rearrange("p n s -> p s n"), AX.X, ALU.max), f_max, t + 1)
                dve.wait_ge(f_cn, 2 * t + 2)
                v.tensor_tensor(cl[par].rearrange("p (n s) -> p n s", s=SL), lg,
                                smx[:, 0:SL].unsqueeze(1).to_broadcast([NP, NE, SL]), ALU.subtract).then_inc(f_sub, 1)

            def combine_sum(t, par, d=None):
                dve.wait_ge(f_exp, t + 1)
                link(dve, v.tensor_reduce(ssum[par], cl[par].rearrange("p (n s) -> p s n", s=SL), AX.X, ALU.add),
                     f_sum, t + 1)
                v.reciprocal(ssum[par], ssum[par]).then_inc(f_rc, 1)

            def combine_stats(t, par, d=None):
                dve.wait_ge(f_y, t + 3)
                link(dve, v.tensor_tensor(yst[par].unsqueeze(1), PS[:, 6 + par:7 + par, 0:D], h1[:, ds(t, 1), :], ALU.add),
                     f_yb, t + 3)
                v.bn_stats(bn6[par], yst[par]).then_inc(f_bn, 1)
                wait_apart(dve, f_bn, 2 * t + 1)
                link(dve, v.bn_aggr(stat[par][:, 0:2], bn6[par]), f_bn, 2 * t + 2)
                v.tensor_scalar(stat[par][:, 2:3], stat[par][:, 1:2], EPS, None, ALU.add).then_inc(f_ve, 1)

            def combine_out(t, par, d):
                dve.wait_ge(f_rs, t + 1)
                dve.wait_ge(d_st[par], 16 * d + 16)
                v.tensor_scalar(hn[par], yst[par], stat[par][:, 0:1], stat[par][:, 3:4], ALU.subtract, ALU.mult
                                ).then_inc(f_o, 1)

            combine_front(0, 0)
            combine_sum(0, 0)
            with dve.Fori(0, TT // 2) as i:
                combine_front(2 * i + 1, 1)
                combine_stats(2 * i, 0)
                combine_sum(2 * i + 1, 1)
                combine_out(2 * i, 0, i)
                combine_front(2 * i + 2, 0)
                combine_stats(2 * i + 1, 1)
                combine_sum(2 * i + 2, 0)
                combine_out(2 * i + 1, 1, i)
            combine_stats(TT - 1, 0)
            combine_out(TT - 1, 0, TT // 2)

        @block.tensor
        def _(pe):
            t_ = nc.tensor
            pe.wait_ge(d_tokw, 16)
            pe.wait_ge(s_const, 9)
            for kc in range(KC):
                for e in range(KD):
                    ins = t_.transpose(PS[:, kc // 2, (kc % 2) * D + e * NP:(kc % 2) * D + (e + 1) * NP],
                                       tokW[:, e, kc * NP:(kc + 1) * NP], ident)
                if kc % 2:
                    ins.then_inc(wt_tr, 1)
            pe.wait_ge(pos_pre, 1)
            for k in range(KD):
                ins = t_.transpose(PS[:, 3, k * T:(k + 1) * T], pos_nat[0:T, k * NP:(k + 1) * NP], ident[0:T, 0:T])
            ins.then_inc(pos_tr, 1)
            pe.wait_ge(wt_cp, 3)
            pe.wait_ge(pos_cp, 1)

            def patches(q, par, d):
                for done in x_ord:
                    pe.wait_ge(done, 2 * q + 2)
                for u in range(2 * KC):
                    kc, half = u // 2, u % 2
                    pe.wait_ge(xt_act if u % 2 == 0 else xt_dve, 6 * q + u // 2 + 1)
                    for w in range(PH):
                        ins = t_.transpose(PS[:, u % 4, w * XP:(w + 1) * XP], xord[par][0:XP, kc, half * PH + w],
                                           ident[0:XP, 0:XP])
                    ins.then_inc(xt_tr, 1)
                pe.wait_ge(xt_act, 2 + 6 * q + 6)
                pe.wait_ge(xt_dve, 2 + 6 * q + 6)
                for j in range(4):
                    e, half = j // 2, j % 2
                    pe.wait_ge(h0_cp, 4 * q + j + 1)
                    for kc in range(KC):
                        ins = t_.matmul(PS[:, 4 + j, 0:PH * XP], tokWT[:, kc, e * NP:(e + 1) * NP],
                                        patchT[par][:, kc, half * PH:(half + 1) * PH, :].rearrange("p w r -> p (w r)"),
                                        start=kc == 0, stop=kc == KC - 1)
                    ins.then_inc(pt_mm, 1)

            tiles(pe, XQ, patches)

            def norm_sum(n, par, d=None):
                pe.wait_ge(n_sq, n + 1)
                pe.wait_ge(n_mx, n + 1)
                for k in range(KD):
                    ins = t_.matmul(PS[:, par, 0:PT], ones, nsq[par][:, k], start=k == 0, stop=k == KD - 1)
                ins.then_inc(n_mm, 1)

            tiles(pe, NPT, norm_sum)
            pe.wait_ge(n_xn, KD * NPT)
            pe.wait_ge(s_setup, 10)

            def project(c):
                par = c % 2
                pe.wait_ge(d_wc[par], 80 * (c // 2 + 1))
                with pe.Fori(0, NPT) as n:
                    u0 = (n + c * NPT) * 4
                    for tag in range(4):
                        pe.wait_ge(pj_cp, u0 + tag + 1)
                        for k in range(KD):
                            if tag < 2:
                                w = wc[par][:, k, 2:4, :].rearrange("p s n -> p (s n)")[:, tag::2]
                            else:
                                w = wc[par][:, k, tag - 2, :]
                            ins = t_.matmul(PS[:, tag, 0:PT], w, xnT[:, k, ds(n * PT, PT)], start=k == 0, stop=k == KD - 1)
                        ins.then_inc(pj_mm, 1)

            def values(n, par, d):
                pe.wait_ge(v_st, n + 1)
                pe.wait_ge(v_cp, n + 1)
                bank = PS[0:GT, 4 + par, :]
                t_.matmul(bank, ones3[0:65, 0:GT], bias3[0:65, NS:NS + INNER], start=True, stop=False)
                for k in range(KD):
                    ins = t_.matmul(bank, xst[par][:, k], wv[:, k], start=False, stop=k == KD - 1)
                ins.then_inc(v_mm, 1)

            def attend(c):
                base = c * NG
                uses = [len(range(b, NG, AB)) for b in range(AB)]

                def front(gi, b, d):
                    n = gi + base
                    pe.wait_ge(d_grp[b], 32 * (d + (c * uses[b] + 1)))
                    pe.wait_ge(a_scp, n + 1)
                    for h in range(2):
                        rows = slice(h * DH, (h + 1) * DH)
                        ins = t_.matmul(PS[0:GT, 4 + h, 0:GT], qkst[b][rows, 1], qkst[b][rows, 0], start=True, stop=True)
                    ins.then_inc(a_s, 1)

                def back(gi, b, d):
                    n = gi + base
                    pe.wait_ge(a_mk, n + 3)
                    pe.wait_ge(a_ocp, n + 1)
                    for h in range(2):
                        ins = t_.matmul(PS[h * DH:(h + 1) * DH, 6 + b % 2, 0:GT], vst[b][0:GT, h * DH:(h + 1) * DH],
                                        smk[b % 2][0:GT, h], start=True, stop=True)
                    ins.then_inc(a_o, 1)

                staggered4(pe, NG, front, back)

            project(0)
            pe.wait_ge(d_wv, 16)
            tiles(pe, NG, values)
            project(1)
            pe.wait_ge(v_cp, 2 + NG)
            for c in range(NC):
                if 1 <= c and c + 1 < NC:
                    project(c + 1)
                if c:
                    attend(c - 1)
            attend(NC - 1)

            pe.wait_ge(d_phi, 16)
            for k in range(KD):
                for s in range(4):
                    if k:
                        pe.wait_ge(ph_cp, s + 1)
                    for b in range(4):
                        ins = t_.transpose(PS[:, s, b * NP:(b + 1) * NP], phi_nat[:, 4 * s + b, k * NP:(k + 1) * NP], ident)
                    ins.then_inc(ph_tr, 1)
            pe.wait_ge(d_wo, 32)

            def out_product(t, par, d):
                pe.wait_ge(d_ost[par], 32 * d + 32)
                pe.wait_ge(o_y, t + 1)
                pe.wait_ge(a_ocp, 2 + NC * NG)
                for k in range(KD):
                    t_.matmul(PS[:, 4 + par, k * NP:(k + 1) * NP], hst[par][:, k], ident, start=k == 0, stop=False,
                              skip_group_check=True)
                for c in range(NC):
                    ins = t_.matmul(PS[:, 4 + par, 0:D], ost[par][:, c], wo[:, c], start=False, stop=c == NC - 1,
                                    skip_group_check=True)
                ins.then_inc(o_mm, 1)

            def out_transpose(t, par, d=None):
                pe.wait_ge(o_h, t + 3)
                pe.wait_ge(o_tc, t + 1)
                for k in range(KD):
                    ins = t_.transpose(PS[:, 6 + par, k * NP:(k + 1) * NP], hn[par][:, k * NP:(k + 1) * NP], ident)
                ins.then_inc(o_tr, 1)

            out_product(0, 0, 0)
            out_product(1, 1, 0)
            with pe.Fori(0, TT // 2 - 1) as i:
                out_product(2 * i + 2, 0, i + 1)
                out_transpose(2 * i, 0)
                out_product(2 * i + 3, 1, i + 1)
                out_transpose(2 * i + 1, 1)
            out_product(TT - 1, 0, TT // 2)
            out_transpose(TT - 3, 0)
            out_transpose(TT - 2, 1)
            out_transpose(TT - 1, 0)

            def logits(bank, col, n_banks, par):
                for s in range(n_banks):
                    cols = slice(col + s * BANK, col + (s + 1) * BANK)
                    t_.matmul(PS[:, bank + s, :], ones3[0:65], bias3[0:65, cols], start=True, stop=False)
                    for k in range(KD):
                        ins = t_.matmul(PS[:, bank + s, :], hst[par][:, k], phiT[:, k, cols], start=False, stop=k == KD - 1)
                return ins

            pe.wait_ge(ph_cp, 8)
            pe.wait_ge(o_y, 2 + TT)
            pe.wait_ge(o_tc, 2 + TT)
            for half in range(2):
                base = half * TT
                if half:
                    pe.wait_ge(x_cp, 4)
                pe.wait_ge(m_sub, 2 + base)
                for b in range(4):
                    t_.matmul(PS[:, 4 + b, :], zeros3[0:1], bias3[0:1, 0:BANK], start=True, stop=False)

                def dispatch_logits(t, par, d):
                    n = t + base
                    pe.wait_ge(d_hst[par], 16 * (half * ((TT + 1) // 2 if par == 0 else TT // 2) + d + 1))
                    pe.wait_ge(m_sub, n + 1)
                    logits(2 * par, half * HS, 2, par).then_inc(m_lg, 1)

                def accumulate(t, par, last=False):
                    pe.wait_ge(m_dn, t + base + 3)
                    for j in range(SC // 2):
                        ins = t_.matmul(PS[:, 4 + j // 2, (j % 2) * D:(j % 2 + 1) * D], dn[par][:, j * NP:(j + 1) * NP],
                                        h1[:, t, :] if last else h1[:, ds(t, 1), :], start=False, stop=False,
                                        skip_group_check=True)
                    if last:
                        for b in range(4):
                            ins = t_.matmul(PS[:, 4 + b, :], zeros3[0:1], bias3[0:1, 0:BANK], start=False, stop=True)
                    ins.then_inc(m_x, 1)

                dispatch_logits(0, 0, 0)
                with pe.Fori(0, TT // 2) as i:
                    dispatch_logits(2 * i + 1, 1, i)
                    accumulate(2 * i, 0)
                    dispatch_logits(2 * i + 2, 0, i + 1)
                    accumulate(2 * i + 1, 1)
                accumulate(TT - 1, 0, last=True)

            pe.wait_ge(d_eb, 16)

            def transpose_slots(j):
                pe.wait_ge(e_th, j + 1)
                pe.wait_ge(e_tc, j + 1)
                for k in range(KD):
                    ins = t_.transpose(PS[:, j % 2, k * NP:(k + 1) * NP], xs[:, j, k * NP:(k + 1) * NP], ident)
                ins.then_inc(e_tr, 1)

            transpose_slots(0)
            for j in range(SC):
                if j + 1 < SC:
                    transpose_slots(j + 1)
                pe.wait_ge(e_tc, j + 3)
                pe.wait_ge(d_we[j % WEB], 32 * (j // WEB + 1))
                pe.wait_ge(e_cp, j + 1)
                bank = PS[:, 2 + j % 2, 0:D]
                for e in range(EC):
                    rows = slice(e * SL, (e + 1) * SL)
                    for k in range(KD):
                        t_.matmul(bank[rows], xtT[j % 2][:, k, rows], we[j % WEB][:, k, e], start=k == 0, stop=False,
                                  skip_group_check=True)
                t_.matmul(bank, chunk_sel[0:EC], eb[0:EC, j], start=False, stop=True, skip_group_check=True).then_inc(e_mm, 1)

            pe.wait_ge(e_cp, 2 + SC)
            hb = [2 * ((TT + 1) // 2), 2 * (TT // 2)]

            def combine_logits(t, par, d):
                pe.wait_ge(d_hst[par], 16 * (d + (hb[par] + 1)))
                pe.wait_ge(f_sub, t + 1)
                logits(0, 0, 4, par).then_inc(f_lg, 1)

            def combine(t, par, d=None):
                pe.wait_ge(f_cn, 2 * t + 6)

                def turn(b):
                    pe.wait_ge(f_tc, 4 * t + b + 1)
                    for j in range(4):
                        s = 4 * b + j
                        ins = t_.transpose(PS[:, 4 + b % 2, j * NP:(j + 1) * NP], cn[par][:, s * NP:(s + 1) * NP], ident)
                    ins.then_inc(f_tr, 1)

                def add(b):
                    if b == 0:
                        pe.wait_ge(f_yb, t + 1)
                    pe.wait_ge(f_tc, 4 * t + b + 3)
                    for j in range(4):
                        s = 4 * b + j
                        ins = t_.matmul(PS[:, 6 + par, 0:D], ct[par][:, s], yt[:, s], start=s == 0, stop=s == SC - 1)
                    return ins

                turn(0)
                turn(1)
                add(0)
                turn(2)
                add(1)
                turn(3)
                add(2)
                add(3).then_inc(f_y, 1)

            combine_logits(0, 0, 0)
            with pe.Fori(0, TT // 2) as i:
                combine_logits(2 * i + 1, 1, i)
                combine(2 * i, 0)
                combine_logits(2 * i + 2, 0, i + 1)
                combine(2 * i + 1, 1)
            combine(TT - 1, 0)


_INS = ['x', 'L0_tok_W', 'L0_tok_b', 'L0_tok_cls_token', 'L0_tok_pos_embed', 'L0_attn_gamma', 'L0_attn_W_qkv',
        'L0_attn_b_qkv', 'L0_attn_W_a', 'L0_attn_b_a', 'L0_attn_W_out', 'L0_attn_b_out', 'L0_ffn_phi_w',
        'L0_ffn_phi_b', 'L0_ffn_expert_w', 'L0_ffn_expert_b']


def kernel(**inputs):
    import numpy as _np
    import concourse.bacc as _bacc
    from concourse import mybir as _mybir
    from concourse.bass_utils import run_bass_kernel_spmd as _run

    nc = _bacc.Bacc("TRN2", target_bir_lowering=False, num_devices=1)
    arrays, args = {}, []
    for name in _INS:
        a = _np.ascontiguousarray(inputs[name])
        arrays[f"in_{name}_dram"] = a
        args.append(nc.dram_tensor(f"in_{name}_dram", a.shape, _mybir.dt.from_np(a.dtype), kind="ExternalInput").ap())
    n_img, n_tok, n_ch = inputs['x'].shape[0], inputs['L0_tok_pos_embed'].shape[1], inputs['L0_tok_W'].shape[0]
    args.append(nc.dram_tensor("out_0_dram", (n_img * n_tok, n_ch), _mybir.dt.float32, kind="ExternalOutput").ap())
    vit_tower_kernel(nc, *args)
    r = _run(nc, [arrays], core_ids=[0])
    return r.results[0]["out_0_dram"].reshape(n_img, n_tok, n_ch)
```
